# Optimizing a Trainium2 kernel written in Bass

```python
import numpy as np
import jax
import jax.numpy as jnp

def _softmax(x, axis=-1):
    return jax.nn.softmax(x, axis=axis)

def _gelu(x):
    return jax.nn.gelu(x, approximate=True)

def _silu(x):
    return jax.nn.silu(x)

def _sigmoid(x):
    return jax.nn.sigmoid(x)

def _layernorm(x, axis=-1, eps=1e-05):
    m = jnp.mean(x, axis=axis, keepdims=True)
    v = jnp.var(x, axis=axis, keepdims=True)
    return (x - m) / jnp.sqrt(v + eps)

def _scatter_add(tgt, idx, src, axis=0):
    return tgt.at[idx].add(src)

def _segment_sum(src, seg, n):
    return jax.ops.segment_sum(src, seg, n)
kernel_name = 'mk_seq_preln_d2_jaxref_r8_53b847'

def setup_inputs(seed: int=0):
    np.random.seed(seed)
    _w = jnp.asarray

    def _L0_attn_setup():
        import jax, jax.numpy as jnp
        import numpy as np
        N_EMBD = 128
        N_HEAD = 16
        HEAD_DIM = N_EMBD // N_HEAD
        KV_RANK = 32
        Q_RANK = 64
        ROPE_DIM = 32
        B, T = (2, 256)
        EPS = 1e-06

        def _rope_tables(T, dim):
            inv_freq = 1.0 / 10000.0 ** (np.arange(0, dim, 2, dtype=np.float32) / dim)
            t = np.arange(T, dtype=np.float32)
            freqs = np.outer(t, inv_freq)
            emb = np.concatenate([freqs, freqs], -1)
            return (jnp.asarray(np.cos(emb)), jnp.asarray(np.sin(emb)))

        def _apply_rope(x, cos, sin):
            d2 = x.shape[-1] // 2
            x1, x2 = (x[..., :d2], x[..., d2:])
            rot = jnp.concatenate([-x2, x1], axis=-1)
            return x * cos[None, None, :, :] + rot * sin[None, None, :, :]
        key = jax.random.key(seed)
        ks = jax.random.split(key, 10)

        def w(k, fan_in, fan_out):
            return jax.random.normal(k, (fan_in, fan_out), dtype=jnp.float32) * fan_in ** (-0.5)
        return {'x': jax.random.normal(ks[0], (B, T, N_EMBD), dtype=jnp.float32), 'W_kv': w(ks[1], N_EMBD, KV_RANK), 'g_kv': jnp.ones((KV_RANK,), dtype=jnp.float32), 'W_kdec': w(ks[2], KV_RANK, N_HEAD * HEAD_DIM), 'W_vdec': w(ks[3], KV_RANK, N_HEAD * HEAD_DIM), 'W_q': w(ks[4], N_EMBD, Q_RANK), 'W_qdec': w(ks[5], Q_RANK, N_HEAD * HEAD_DIM), 'W_krope': w(ks[6], N_EMBD, N_HEAD * ROPE_DIM), 'W_qrope': w(ks[7], Q_RANK, N_HEAD * ROPE_DIM), 'W_o': w(ks[8], N_HEAD * HEAD_DIM, N_EMBD)}
    _L0_attn_in = _L0_attn_setup()

    def _L0_ffn_setup():
        import jax, jax.numpy as jnp
        import numpy as np
        B, S, DIM, FFN, E = (4, 256, 128, 512, 8)
        key = jax.random.key(seed)
        k0, k1, k2, k3 = jax.random.split(key, 4)
        scale = 0.02
        return {'hidden_states': jax.random.normal(k0, (B, S, DIM), jnp.float32), 'router_w': jax.random.normal(k1, (DIM, E), jnp.float32) * scale, 'router_b': jnp.zeros((E,), jnp.float32), 'w1': jax.random.normal(k2, (E, DIM, 2 * FFN), jnp.float32) * scale, 'w2': jax.random.normal(k3, (E, FFN, DIM), jnp.float32) * scale}
    _L0_ffn_in = _L0_ffn_setup()

    def _L1_attn_setup():
        import jax, jax.numpy as jnp
        import numpy as np
        OFFSETS = np.array(sorted(set(range(0, 33)) | {48, 64, 96, 128, 192, 32, 48, 64, 96, 128, 192}), dtype=np.int32)
        NUM_HEADS = 16
        key = jax.random.key(seed)
        ks = jax.random.split(key, 8)
        B, N, D = (1, 256, 128)
        H = NUM_HEADS
        O = len(OFFSETS)
        s = 0.02
        x = jax.random.normal(ks[0], (B, N, D), dtype=jnp.float32)
        Wqkv = jax.random.normal(ks[1], (3 * D, D), dtype=jnp.float32) * s
        bqkv = jnp.zeros((3 * D,), dtype=jnp.float32)
        Wout = jax.random.normal(ks[2], (D, D), dtype=jnp.float32) * s
        bout = jnp.zeros((D,), dtype=jnp.float32)
        Wgate = jax.random.normal(ks[3], (D, D), dtype=jnp.float32) * s
        bgate = jnp.full((D,), 2.0, dtype=jnp.float32)
        alphas = jnp.linspace(0.2, 2.0, H)
        delta = jnp.log1p(jnp.asarray(OFFSETS, dtype=jnp.float32))
        pos_bias = -delta[:, None] * alphas[None, :]
        return {'x': x, 'Wqkv': Wqkv, 'bqkv': bqkv, 'Wout': Wout, 'bout': bout, 'Wgate': Wgate, 'bgate': bgate, 'pos_bias': pos_bias}
    _L1_attn_in = _L1_attn_setup()

    def _L1_ffn_setup():
        import jax, jax.numpy as jnp
        import numpy as np
        from jax.scipy.linalg import expm
        B, S, D, E, K, NROT = (2, 256, 128, 8, 2, 3)
        EPS = 1e-05

        def _gelu(x):
            return jax.nn.gelu(x, approximate=False)

        def _forward(x, ln_gamma, ln_beta, abel_w, abel_b, moe_gate_w, moe_gate_b, ew1, eb1, ew2, eb2, gens, gc_w, gc_b):
            residual = x
            mu = jnp.mean(x, axis=-1, keepdims=True)
            var = jnp.mean((x - mu) ** 2, axis=-1, keepdims=True)
            xn = (x - mu) * jax.lax.rsqrt(var + EPS) * ln_gamma + ln_beta
            abel_out = _gelu(xn @ abel_w + abel_b)
            logits = xn @ moe_gate_w + moe_gate_b
            topw, topi = jax.lax.top_k(logits, K)
            topw = jax.nn.softmax(topw, axis=-1)
            w_dense = jnp.sum(jax.nn.one_hot(topi, E, dtype=xn.dtype) * topw[..., None], axis=-2)
            h = _gelu(jnp.einsum('bsd,edh->ebsh', xn, ew1) + eb1[:, None, None, :])
            eo = jnp.einsum('ebsh,ehd->ebsd', h, ew2) + eb2[:, None, None, :]
            moe_out = jnp.einsum('ebsd,bse->bsd', eo, w_dense)
            for i in range(NROT):
                moe_out = moe_out @ expm(gens[i])
            combined = jnp.concatenate([abel_out, moe_out], axis=-1)
            gate = jax.nn.sigmoid(combined @ gc_w + gc_b)
            mixed = abel_out * (1.0 - gate) + moe_out * gate
            return residual + mixed
        key = jax.random.key(seed)
        ks = jax.random.split(key, 16)
        sc = 0.02
        x = jax.random.normal(ks[0], (B, S, D), jnp.float32)
        ln_gamma = 1.0 + sc * jax.random.normal(ks[1], (D,), jnp.float32)
        ln_beta = sc * jax.random.normal(ks[2], (D,), jnp.float32)
        abel_w = sc * jax.random.normal(ks[3], (D, D), jnp.float32)
        abel_b = sc * jax.random.normal(ks[4], (D,), jnp.float32)
        moe_gate_w = sc * jax.random.normal(ks[5], (D, E), jnp.float32)
        moe_gate_b = sc * jax.random.normal(ks[6], (E,), jnp.float32)
        ew1 = sc * jax.random.normal(ks[7], (E, D, 2 * D), jnp.float32)
        eb1 = sc * jax.random.normal(ks[8], (E, 2 * D), jnp.float32)
        ew2 = sc * jax.random.normal(ks[9], (E, 2 * D, D), jnp.float32)
        eb2 = sc * jax.random.normal(ks[10], (E, D), jnp.float32)
        g = sc * jax.random.normal(ks[11], (NROT, D, D), jnp.float32)
        gens = 0.5 * (g - jnp.swapaxes(g, -1, -2))
        gc_w = sc * jax.random.normal(ks[12], (2 * D, 1), jnp.float32)
        gc_b = sc * jax.random.normal(ks[13], (1,), jnp.float32)
        return dict(x=x, ln_gamma=ln_gamma, ln_beta=ln_beta, abel_w=abel_w, abel_b=abel_b, moe_gate_w=moe_gate_w, moe_gate_b=moe_gate_b, ew1=ew1, eb1=eb1, ew2=ew2, eb2=eb2, gens=gens, gc_w=gc_w, gc_b=gc_b)
    _L1_ffn_in = _L1_ffn_setup()
    _d = {'L0_attn_x': _L0_attn_in['x'], 'L0_attn_W_kv': _L0_attn_in['W_kv'], 'L0_attn_g_kv': _L0_attn_in['g_kv'], 'L0_attn_W_kdec': _L0_attn_in['W_kdec'], 'L0_attn_W_vdec': _L0_attn_in['W_vdec'], 'L0_attn_W_q': _L0_attn_in['W_q'], 'L0_attn_W_qdec': _L0_attn_in['W_qdec'], 'L0_attn_W_krope': _L0_attn_in['W_krope'], 'L0_attn_W_qrope': _L0_attn_in['W_qrope'], 'L0_attn_W_o': _L0_attn_in['W_o'], 'L0_ffn_router_w': _L0_ffn_in['router_w'], 'L0_ffn_router_b': _L0_ffn_in['router_b'], 'L0_ffn_w1': _L0_ffn_in['w1'], 'L0_ffn_w2': _L0_ffn_in['w2'], 'L1_attn_Wqkv': _L1_attn_in['Wqkv'], 'L1_attn_bqkv': _L1_attn_in['bqkv'], 'L1_attn_Wout': _L1_attn_in['Wout'], 'L1_attn_bout': _L1_attn_in['bout'], 'L1_attn_Wgate': _L1_attn_in['Wgate'], 'L1_attn_bgate': _L1_attn_in['bgate'], 'L1_attn_pos_bias': _L1_attn_in['pos_bias'], 'L1_ffn_ln_gamma': _L1_ffn_in['ln_gamma'], 'L1_ffn_ln_beta': _L1_ffn_in['ln_beta'], 'L1_ffn_abel_w': _L1_ffn_in['abel_w'], 'L1_ffn_abel_b': _L1_ffn_in['abel_b'], 'L1_ffn_moe_gate_w': _L1_ffn_in['moe_gate_w'], 'L1_ffn_moe_gate_b': _L1_ffn_in['moe_gate_b'], 'L1_ffn_ew1': _L1_ffn_in['ew1'], 'L1_ffn_eb1': _L1_ffn_in['eb1'], 'L1_ffn_ew2': _L1_ffn_in['ew2'], 'L1_ffn_eb2': _L1_ffn_in['eb2'], 'L1_ffn_gens': _L1_ffn_in['gens'], 'L1_ffn_gc_w': _L1_ffn_in['gc_w'], 'L1_ffn_gc_b': _L1_ffn_in['gc_b']}
    _x0 = _d['L0_attn_x']
    _d['L0_attn_x'] = jax.random.normal(jax.random.fold_in(jax.random.key(seed), 1), (4, 1024, 128), dtype=_x0.dtype)
    del _x0
    return _d

def reference(L0_attn_x, L0_attn_W_kv, L0_attn_g_kv, L0_attn_W_kdec, L0_attn_W_vdec, L0_attn_W_q, L0_attn_W_qdec, L0_attn_W_krope, L0_attn_W_qrope, L0_attn_W_o, L0_ffn_router_w, L0_ffn_router_b, L0_ffn_w1, L0_ffn_w2, L1_attn_Wqkv, L1_attn_bqkv, L1_attn_Wout, L1_attn_bout, L1_attn_Wgate, L1_attn_bgate, L1_attn_pos_bias, L1_ffn_ln_gamma, L1_ffn_ln_beta, L1_ffn_abel_w, L1_ffn_abel_b, L1_ffn_moe_gate_w, L1_ffn_moe_gate_b, L1_ffn_ew1, L1_ffn_eb1, L1_ffn_ew2, L1_ffn_eb2, L1_ffn_gens, L1_ffn_gc_w, L1_ffn_gc_b):

    def _L0_attn_ref(x, W_kv, g_kv, W_kdec, W_vdec, W_q, W_qdec, W_krope, W_qrope, W_o):
        import jax, jax.numpy as jnp
        import numpy as np
        N_EMBD = 128
        N_HEAD = 16
        HEAD_DIM = N_EMBD // N_HEAD
        KV_RANK = 32
        Q_RANK = 64
        ROPE_DIM = 32
        B, T = (2, 256)
        EPS = 1e-06

        def _rope_tables(T, dim):
            inv_freq = 1.0 / 10000.0 ** (np.arange(0, dim, 2, dtype=np.float32) / dim)
            t = np.arange(T, dtype=np.float32)
            freqs = np.outer(t, inv_freq)
            emb = np.concatenate([freqs, freqs], -1)
            return (jnp.asarray(np.cos(emb)), jnp.asarray(np.sin(emb)))

        def _apply_rope(x, cos, sin):
            d2 = x.shape[-1] // 2
            x1, x2 = (x[..., :d2], x[..., d2:])
            rot = jnp.concatenate([-x2, x1], axis=-1)
            return x * cos[None, None, :, :] + rot * sin[None, None, :, :]
        Bx, Tx, C = x.shape
        kv_c = x @ W_kv
        kv_c = kv_c * jax.lax.rsqrt(jnp.mean(kv_c * kv_c, axis=-1, keepdims=True) + EPS) * g_kv
        q_c = x @ W_q

        def heads(y, d):
            return y.reshape(Bx, Tx, N_HEAD, d).transpose(0, 2, 1, 3)
        k_content = heads(kv_c @ W_kdec, HEAD_DIM)
        v = heads(kv_c @ W_vdec, HEAD_DIM)
        q_content = heads(q_c @ W_qdec, HEAD_DIM)
        k_rope = heads(x @ W_krope, ROPE_DIM)
        q_rope = heads(q_c @ W_qrope, ROPE_DIM)
        cos, sin = _rope_tables(Tx, ROPE_DIM)
        q_rope = _apply_rope(q_rope, cos, sin)
        k_rope = _apply_rope(k_rope, cos, sin)
        q = jnp.concatenate([q_content, q_rope], axis=-1)
        k = jnp.concatenate([k_content, k_rope], axis=-1)
        scale = 1.0 / jnp.sqrt(jnp.float32(q.shape[-1]))
        scores = jnp.einsum('bhqd,bhkd->bhqk', q, k) * scale
        causal = jnp.tril(jnp.ones((Tx, Tx), dtype=bool))
        scores = jnp.where(causal[None, None], scores, jnp.float32(-jnp.inf))
        attn = jax.nn.softmax(scores, axis=-1)
        out = jnp.einsum('bhqk,bhkd->bhqd', attn, v)
        out = out.transpose(0, 2, 1, 3).reshape(Bx, Tx, N_HEAD * HEAD_DIM)
        return out @ W_o

    def _L0_ffn_ref(hidden_states, router_w, router_b, w1, w2):
        import jax, jax.numpy as jnp
        import numpy as np
        B, S, DIM, FFN, E = (4, 256, 128, 512, 8)
        b, s, d = hidden_states.shape
        x = hidden_states.reshape(-1, d)
        logits = x @ router_w + router_b
        route = jax.nn.softmax(logits, axis=1)
        max_prob = jnp.max(route, axis=1, keepdims=True)
        max_ind = jnp.argmax(route, axis=1)
        out = jnp.zeros_like(x)
        num_experts = w1.shape[0]
        for e in range(num_experts):
            h = x @ w1[e]
            a, g = jnp.split(h, 2, axis=1)
            y = jax.nn.silu(a) * g @ w2[e]
            out = jnp.where((max_ind == e)[:, None], y, out)
        out = out * max_prob
        return out.reshape(b, s, d)

    def _L1_attn_ref(x, Wqkv, bqkv, Wout, bout, Wgate, bgate, pos_bias):
        import jax, jax.numpy as jnp
        import numpy as np
        OFFSETS = np.array(sorted(set(range(0, 33)) | {48, 64, 96, 128, 192, 32, 48, 64, 96, 128, 192}), dtype=np.int32)
        NUM_HEADS = 16
        B, N, D = x.shape
        H = NUM_HEADS
        HD = D // H
        offs = jnp.asarray(OFFSETS)
        max_off = int(OFFSETS[-1])
        scale = HD ** (-0.5)
        qkv = x @ Wqkv.T + bqkv
        q, k, v = jnp.split(qkv, 3, axis=-1)
        q = q.reshape(B, N, H, HD).transpose(0, 2, 1, 3)
        k = k.reshape(B, N, H, HD).transpose(0, 2, 1, 3)
        v = v.reshape(B, N, H, HD).transpose(0, 2, 1, 3)
        k_pad = jnp.pad(k, ((0, 0), (0, 0), (max_off, 0), (0, 0)))
        v_pad = jnp.pad(v, ((0, 0), (0, 0), (max_off, 0), (0, 0)))
        n_idx = jnp.arange(N)
        gather_idx = max_off - offs[:, None] + n_idx[None, :]
        K_all = k_pad[:, :, gather_idx, :]
        V_all = v_pad[:, :, gather_idx, :]
        scores = jnp.einsum('bhnd,bhond->bhno', q, K_all) * scale
        scores = scores + pos_bias.T[None, :, None, :]
        invalid = n_idx[:, None] < offs[None, :]
        scores = jnp.where(invalid[None, None], -jnp.inf, scores)
        alpha = jax.nn.softmax(scores, axis=-1)
        out = jnp.einsum('bhno,bhond->bhnd', alpha, V_all)
        flat = out.transpose(0, 2, 1, 3).reshape(B, N, D)
        gate = jax.nn.sigmoid(x @ Wgate.T + bgate)
        return flat * gate @ Wout.T + bout

    def _L1_ffn_ref(x, ln_gamma, ln_beta, abel_w, abel_b, moe_gate_w, moe_gate_b, ew1, eb1, ew2, eb2, gens, gc_w, gc_b):
        import jax, jax.numpy as jnp
        import numpy as np
        from jax.scipy.linalg import expm
        B, S, D, E, K, NROT = (2, 256, 128, 8, 2, 3)
        EPS = 1e-05

        def _gelu(x):
            return jax.nn.gelu(x, approximate=False)

        def _forward(x, ln_gamma, ln_beta, abel_w, abel_b, moe_gate_w, moe_gate_b, ew1, eb1, ew2, eb2, gens, gc_w, gc_b):
            residual = x
            mu = jnp.mean(x, axis=-1, keepdims=True)
            var = jnp.mean((x - mu) ** 2, axis=-1, keepdims=True)
            xn = (x - mu) * jax.lax.rsqrt(var + EPS) * ln_gamma + ln_beta
            abel_out = _gelu(xn @ abel_w + abel_b)
            logits = xn @ moe_gate_w + moe_gate_b
            topw, topi = jax.lax.top_k(logits, K)
            topw = jax.nn.softmax(topw, axis=-1)
            w_dense = jnp.sum(jax.nn.one_hot(topi, E, dtype=xn.dtype) * topw[..., None], axis=-2)
            h = _gelu(jnp.einsum('bsd,edh->ebsh', xn, ew1) + eb1[:, None, None, :])
            eo = jnp.einsum('ebsh,ehd->ebsd', h, ew2) + eb2[:, None, None, :]
            moe_out = jnp.einsum('ebsd,bse->bsd', eo, w_dense)
            for i in range(NROT):
                moe_out = moe_out @ expm(gens[i])
            combined = jnp.concatenate([abel_out, moe_out], axis=-1)
            gate = jax.nn.sigmoid(combined @ gc_w + gc_b)
            mixed = abel_out * (1.0 - gate) + moe_out * gate
            return residual + mixed
        return _forward(x, ln_gamma, ln_beta, abel_w, abel_b, moe_gate_w, moe_gate_b, ew1, eb1, ew2, eb2, gens, gc_w, gc_b)
    x = L0_attn_x
    x = x + _L0_attn_ref(_layernorm(x, axis=-1), L0_attn_W_kv, L0_attn_g_kv, L0_attn_W_kdec, L0_attn_W_vdec, L0_attn_W_q, L0_attn_W_qdec, L0_attn_W_krope, L0_attn_W_qrope, L0_attn_W_o)
    x = x + _L0_ffn_ref(_layernorm(x, axis=-1), L0_ffn_router_w, L0_ffn_router_b, L0_ffn_w1, L0_ffn_w2)
    x = x + _L1_attn_ref(_layernorm(x, axis=-1), L1_attn_Wqkv, L1_attn_bqkv, L1_attn_Wout, L1_attn_bout, L1_attn_Wgate, L1_attn_bgate, L1_attn_pos_bias)
    x = x + _L1_ffn_ref(_layernorm(x, axis=-1), L1_ffn_ln_gamma, L1_ffn_ln_beta, L1_ffn_abel_w, L1_ffn_abel_b, L1_ffn_moe_gate_w, L1_ffn_moe_gate_b, L1_ffn_ew1, L1_ffn_eb1, L1_ffn_ew2, L1_ffn_eb2, L1_ffn_gens, L1_ffn_gc_w, L1_ffn_gc_b)
    return x

_drawn_inputs = setup_inputs


def setup_inputs(seed=0):
    import zlib

    import numpy as np

    out = dict(_drawn_inputs(seed))
    spreads = {'L0_attn_g_kv': (1.0, 0.2),
     'L0_ffn_router_b': (0.0, 0.8),
     'L1_attn_bqkv': (0.0, 0.395),
     'L1_attn_bout': (0.0, 0.1),
     'L1_attn_bgate': (2.0, 0.6)}
    factors = {'L0_ffn_router_w': 8.0,
     'L0_ffn_w1': 8.0,
     'L0_ffn_w2': 8.0,
     'L1_attn_Wqkv': 3.124,
     'L1_attn_Wgate': 8.0,
     'L1_attn_pos_bias': 3.351,
     'L1_ffn_ln_gamma': 8.0,
     'L1_ffn_ln_beta': 8.0,
     'L1_ffn_abel_b': 30.38,
     'L1_ffn_moe_gate_w': 8.0,
     'L1_ffn_moe_gate_b': 8.0,
     'L1_ffn_ew1': 8.0,
     'L1_ffn_eb1': 8.0,
     'L1_ffn_ew2': 8.0,
     'L1_ffn_eb2': 52.195,
     'L1_ffn_gens': 8.0,
     'L1_ffn_gc_w': 8.0}
    for name, (base, spread) in spreads.items():
        noise = np.random.default_rng([zlib.crc32(name.encode()), seed]).standard_normal(out[name].shape)
        drawn = base * np.exp(spread * noise) if base else spread * noise
        out[name] = jnp.asarray(drawn.astype(out[name].dtype))
    for name, factor in factors.items():
        out[name] = (out[name] * factor).astype(out[name].dtype)
    return out
```

```python
import numpy as np
import concourse.bass as bass
from concourse import mybir
from contextlib import ExitStack

F32 = mybir.dt.float32
F32R = mybir.dt.float32r
BF16 = mybir.dt.bfloat16
U32 = mybir.dt.uint32
ALU = mybir.AluOpType
ACT = mybir.ActivationFunctionType
AX = mybir.AxisListType

B, T, D = 4, 1024, 128
NT = B * T // 128
OFFS = sorted(set(range(33)) | {48, 64, 96, 128, 192})
NEG = -1.0e30


class Queue:

    def __init__(self, sem, one_by_one=False):
        self.sem, self.ops, self.n, self.waited = sem, [], 0, {}
        self.one_by_one = one_by_one

    def wait(self, *marks):
        for m in marks:
            if m is not None and self.waited.get(m[0].name, 0) < m[1]:
                self.waited[m[0].name] = m[1]
                self.ops.append((None, m, None))

    def do(self, fn, *args, inc=True, **kw):
        if self.one_by_one and self.n:
            self.wait((self.sem, self.n))
        self.ops.append((fn, args, kw, (self.sem, 1) if inc else None))
        self.n += inc
        return (self.sem, self.n)

    def dma(self, fn, dst, src, stream):
        stream[1] += 16
        self.ops.append((fn, (dst, src), {}, (stream[0], 16)))
        return (stream[0], stream[1])

    def play(self, eng):
        for op in self.ops:
            if op[0] is None:
                eng.wait_ge(op[1][0], op[1][1])
            else:
                ins = op[0](*op[1], **op[2])
                if op[3]:
                    ins.then_inc(*op[3])


def run_beside(main, side, ratio):
    k = 0.0
    alive = True
    for _ in main:
        k += 1.0
        while alive and k >= ratio:
            k -= ratio
            try:
                next(side)
            except StopIteration:
                alive = False
    for _ in side:
        pass


def program(nc, a, out, stop=9):
    ctx = ExitStack()

    def sem(name):
        return ctx.enter_context(nc.semaphore(name))

    pe, dve, act, pool, sp = (Queue(sem(n)) for n in ("s_pe", "s_dve", "s_act", "s_pool", "s_sp"))
    pool.one_by_one = True
    te, ve, se, ge, ye = nc.tensor, nc.vector, nc.scalar, nc.gpsimd, nc.sync

    def stream(name):
        return [sem(name), 0]

    def sb(st, name, shape, dt=F32):
        return st.enter_context(nc.sbuf_tensor(name, shape, dt))

    def barrier():
        last = [(q.sem, q.n) for q in (pe, dve, act, pool)]
        for q in (pe, dve, act, pool, sp):
            q.wait(*[m for m in last if m[1]])

    S = [ctx.enter_context(nc.psum_tensor(f"S{i}", [128, 1024], F32)) for i in range(3)]
    A = [ctx.enter_context(nc.psum_tensor(f"A{i}", [128, 512], F32)) for i in range(2)]
    s_free, a_free = [()] * 3, [()] * 2
    turn = {"s": 0, "a": 0}

    def take_s():
        i = turn["s"] % 3
        turn["s"] += 1
        pe.wait(*s_free[i])
        return i

    def take_a():
        i = turn["a"] % 2
        turn["a"] += 1
        pe.wait(*a_free[i])
        return i

    x = sb(ctx, "x", [128, NT, D])
    ident = sb(ctx, "ident", [128, 128])
    identb = sb(ctx, "identb", [128, 128], BF16)
    st_x = stream("d_x")
    st_c = stream("d_c")
    x_in = a["x"].rearrange("(n p) d -> p n d", p=128)
    x_done = [sp.dma(ye.dma_start, x[:, 8 * b:8 * b + 8, :], x_in[:, 8 * b:8 * b + 8, :], st_x) for b in range(1)]
    c_id = sp.dma(ye.dma_start, ident[:], a["ident"], stream("d_id"))
    dve.wait(c_id)
    m_idb = dve.do(ve.tensor_copy, identb[:], ident[:])
    x_ready = [x_done[0]] * B

    stats = sb(ctx, "stats", [128, 8, 6])
    mv = sb(ctx, "mv", [128, 8, 2])
    rs = sb(ctx, "rs", [128, 8])
    half = sb(ctx, "half", [128, 8])
    m_half = pool.do(ge.memset, half[:], -0.5)

    def rstd(var_ap, eps, n, ready):
        pool.wait(ready, m_half)
        m = pool.do(ge.tensor_scalar, rs[:, 0:n], var_ap, eps, 1.0, ALU.add, ALU.mult)
        pool.wait(m)
        return pool.do(ge.tensor_tensor, rs[:, 0:n], rs[:, 0:n], half[:, 0:n], ALU.pow)

    def layernorm(src, dst, n, eps, ready, dst_free=()):
        dve.wait(*ready)
        for i in range(n):
            m = dve.do(ve.bn_stats, stats[:, i, :], src[:, i, :])
        dve.wait(m)
        for i in range(n):
            m = dve.do(ve.bn_aggr, mv[:, i, :], stats[:, i, :])
        r = rstd(mv[:, 0:n, 1], eps, n, m)
        dve.wait(m, r, *dst_free)
        for i in range(n):
            m = dve.do(ve.tensor_scalar, dst[:, i, :], src[:, i, :], mv[:, i, 0:1], rs[:, i:i + 1],
                       ALU.subtract, ALU.mult)
        return m

    def transposed(src, dst, n, ready, dst_free=()):
        s = take_s()
        pe.wait(ready, c_id)
        for i in range(n):
            m = pe.do(te.transpose, S[s][:, 128 * i:128 * i + 128], src[:, i, :], ident[:], inc=(i == n - 1))
        act.wait(m, *dst_free)
        m = act.do(se.activation, dst[:, 0:128 * n], S[s][:, 0:128 * n], ACT.Copy)
        s_free[s] = (m,)
        return m

    with ExitStack() as ph:
        t1, t2, t3 = (sb(ph, n, [128, 512]) for n in ("t1", "t2", "t3"))
        names = ("wq", "wqd", "wkd", "wvd", "wo0")
        W = {n: sb(ph, n, [128, 128]) for n in names}
        wkv = sb(ph, "wkv", [128, 32])
        gkv = sb(ph, "gkv", [128, 1])
        R = {n: sb(ph, n, [128, 512]) for n in ("wqA", "wqB", "wkA", "wkB")}
        cos, sin = sb(ph, "cos", [128, T]), sb(ph, "sin", [128, T])
        mkqb, mqkb = sb(ph, "mkqb", [128, 128], BF16), sb(ph, "mqkb", [128, 128], BF16)
        for n in names:
            sp.dma(ye.dma_start, W[n][:], a[n], st_c)
        for n in R:
            sp.dma(ye.dma_start, R[n][:], a[n], st_c)
        sp.dma(ye.dma_start, wkv[:], a["wkv"], st_c)
        sp.dma(ye.dma_start, gkv[:], a["gkv"], st_c)
        sp.dma(ye.dma_start, cos[:], a["cos"], st_c)
        sp.dma(ye.dma_start, sin[:], a["sin"], st_c)
        sp.dma(ye.dma_start, t1[:, 0:128], a["mkq"], st_c)
        w0 = sp.dma(ye.dma_start, t2[:, 0:128], a["mqk"], st_c)
        st_x2 = stream("d_x2")
        for b in range(1, B):
            m = sp.dma(ye.dma_start, x[:, 8 * b:8 * b + 8, :], x_in[:, 8 * b:8 * b + 8, :], st_x2)
        x_ready = [x_ready[0]] + [m] * (B - 1)

        xn = sb(ph, "xn", [128, 8, 128])
        xnT = sb(ph, "xnT", [128, T])
        qc = sb(ph, "qc", [128, T])
        kvs = sb(ph, "kvs", [128, 8, 32])
        kvT = sb(ph, "kvT", [128, T])
        CH = {n: sb(ph, n, [128, T], F32R) for n in ("cqh", "cql", "ckh", "ckl")}
        rh, rl = sb(ph, "rh", [128, T], F32R), sb(ph, "rl", [128, T], F32R)
        Qp = [sb(ph, f"Qp{i}", [128, 4, T], F32R) for i in range(2)]
        Kp = [sb(ph, f"Kp{i}", [128, 4, T], F32R) for i in range(2)]
        V2 = [sb(ph, f"V{i}", [128, 8, 16, 32]) for i in range(2)]
        v_free = [(), ()]
        NP = 4
        P = [sb(ph, f"P{i}", [128, 2, 512]) for i in range(NP)]
        p_free = [()] * NP
        mx = sb(ph, "mx", [128, 8, 4])
        mT = sb(ph, "mT", [4, T], F32R)
        oT = sb(ph, "oT", [128, 512])
        rec = sb(ph, "rec", [128, 4, 4])
        at = sb(ph, "at", [128, 8, 128])
        aT = sb(ph, "aT", [128, 512])

        dve.wait(w0)
        dve.do(ve.tensor_copy, mkqb[:], t1[:, 0:128])
        m_mask = dve.do(ve.tensor_copy, mqkb[:], t2[:, 0:128])
        dve.do(ve.tensor_scalar, W["wkd"][:], W["wkd"][:], gkv[:, 0:1], None, ALU.mult)
        m_w = dve.do(ve.tensor_scalar, W["wvd"][:], W["wvd"][:], gkv[:, 0:1], None, ALU.mult)
        m_z = pool.do(ge.memset, kvT[:], 0.0)
        for V in V2:
            pool.do(ge.memset, V[:], 0.0)
            m_v0 = pool.do(ge.memset, V[:, :, :, 8:9], 1.0)
        for i in range(2):
            m_one = pool.do(ge.memset, Kp[i][96:128, :, :].bitcast(F32), 1.0)

        st_q = [stream(f"d_q{i}") for i in range(2)]
        st_m = [stream(f"d_m{i}") for i in range(2)]
        free = {n: () for n in ("xnT", "qc", "kvT", "cq", "ck", "t1", "t2", "t3", "rh", "rl", "mT", "oT", "at", "aT", "kvn", "xn", "mx")}
        unit_free = [(), ()]
        proj = {}

        def batch_projection(b):
            xb = x[:, 8 * b:8 * b + 8, :]
            m = layernorm(xb, xn, 8, 1e-5, [x_ready[b]], free["xn"])
            yield
            m_t = transposed(xn, xnT, 8, m, free["xnT"])
            free["xn"] = (m_t,)
            yield
            s = take_s()
            pe.wait(m_t, w0)
            for i in range(2):
                m = pe.do(te.matmul, S[s][:, 512 * i:512 * i + 512], W["wq"][:], xnT[:, 512 * i:512 * i + 512],
                          start=True, stop=True, inc=(i == 1))
            act.wait(m, *free["qc"])
            m_qc = act.do(se.activation, qc[:], S[s][:], ACT.Copy)
            s_free[s] = (m_qc,)
            yield
            s = take_s()
            for i in range(8):
                m = pe.do(te.matmul, S[s][:, 32 * i:32 * i + 32], xnT[:, 128 * i:128 * i + 128], wkv[:],
                          start=True, stop=True, inc=(i == 7))
            kv = S[s][:, 0:256].rearrange("p (n d) -> p n d", d=32)
            act.wait(m)
            m_sq = act.do(se.activation, kvs[:], kv, ACT.Square)
            dve.wait(m_sq)
            m = dve.do(ve.tensor_reduce, mv[:, :, 1], kvs[:], AX.X, ALU.add)
            pool.wait(m)
            m = pool.do(ge.tensor_scalar, mv[:, :, 1], mv[:, :, 1], 1.0 / 32, 1.0, ALU.mult, ALU.mult)
            m_r = rstd(mv[:, :, 1], 1e-6, 8, m)
            dve.wait(m_r)
            m_kv = dve.do(ve.tensor_tensor, kvs[:], kv, rs[:, :, None].broadcast_to([128, 8, 32]), ALU.mult)
            s_free[s] = (m_sq, m_kv)
            yield
            s = take_s()
            pe.wait(m_kv)
            for i in range(8):
                m = pe.do(te.transpose, S[s][0:32, 128 * i:128 * i + 128], kvs[:, i, :], ident[:], inc=(i == 7))
            act.wait(m, m_z, *free["kvT"])
            m_kvT = act.do(se.activation, kvT[0:32, :], S[s][0:32, :], ACT.Copy)
            s_free[s] = (m_kvT,)
            yield
            for n, w, src, ready in (("cq", "wqd", qc, m_qc), ("ck", "wkd", kvT, m_kvT)):
                s = take_s()
                pe.wait(ready, m_w)
                for i in range(2):
                    m = pe.do(te.matmul, S[s][:, 512 * i:512 * i + 512], W[w][:], src[:, 512 * i:512 * i + 512],
                              start=True, stop=True, inc=(i == 1))
                act.wait(m, *free[n])
                m_h = act.do(se.activation, CH[n + "h"][:], S[s][:], ACT.Copy)
                dve.wait(m_h, *free[n])
                m_l = dve.do(ve.tensor_tensor, CH[n + "l"][:], S[s][:], CH[n + "h"][:].bitcast(F32), ALU.subtract)
                s_free[s] = (m_h, m_l)
                proj[n] = (m_h, m_l)
                yield
            s = take_s()
            for i in range(8):
                m = pe.do(te.matmul, S[s][:, 128 * i:128 * i + 128], kvT[:, 128 * i:128 * i + 128], W["wvd"][:],
                          start=True, stop=True, inc=(i == 7))
            free["kvT"] = (m,)
            dve.wait(m, m_v0, *v_free[b % 2])
            m_v = dve.do(ve.tensor_copy, V2[b % 2][:, :, :, 0:8],
                         S[s][:, :].rearrange("p (n h d) -> p n h d", n=8, h=16))
            s_free[s] = (m_v,)
            proj[("V", b)] = m_v
            proj["x"] = m_t
            proj["qc"] = m_qc
            yield

        def rope(u, g, name, wa, wb, src, ready, dst, order, fresh):
            for i in range(2):
                c = slice(512 * i, 512 * i + 512)
                s = take_s()
                pe.wait(ready)
                pe.do(te.matmul, S[s][:, 0:512], R[wa][:, 128 * g:128 * g + 128], src[:, c], start=True, stop=True, inc=False)
                m = pe.do(te.matmul, S[s][:, 512:1024], R[wb][:, 128 * g:128 * g + 128], src[:, c], start=True, stop=True)
                dve.wait(m, *free["t1"], *free["t2"])
                m_1 = dve.do(ve.tensor_tensor, t1[:], S[s][:, 0:512], cos[:, c], ALU.mult)
                m_2 = dve.do(ve.tensor_tensor, t2[:], S[s][:, 512:1024], sin[:, c], ALU.mult)
                s_free[s] = (m_2,)
                pool.wait(m_2, *free["t3"])
                m_3 = pool.do(ge.tensor_tensor, t3[:], t1[:], t2[:], ALU.add)
                free["t1"] = free["t2"] = (m_3,)
                act.wait(m_3, *free["rh"])
                m_h = act.do(se.activation, rh[:, c], t3[:], ACT.Copy)
                pool.wait(m_h, *free["rl"])
                m_l = pool.do(ge.tensor_tensor, rl[:, c], t3[:], rh[:, c].bitcast(F32), ALU.subtract)
                free["t3"] = (m_l,)
                yield
            hi, lo = rh[:].bitcast(F32), rl[:].bitcast(F32)
            sp.wait(m_h, m_l, *fresh)
            for h in range(4):
                for k, part in enumerate(order):
                    m = sp.dma(ye.dma_start, dst[32 * k:32 * k + 32, h, :].bitcast(F32),
                               (hi if part == "h" else lo)[32 * h:32 * h + 32, :], st_q[u % 2])
            ch = {"h": CH[name + "h"][:].bitcast(F32), "l": CH[name + "l"][:].bitcast(F32)}
            sp.wait(*proj[name])
            for h in range(4):
                p = 8 * (4 * g + h)
                for k, part in enumerate(order):
                    m = sp.dma(ye.dma_start, dst[96 + 8 * k:104 + 8 * k, h, :].bitcast(F32), ch[part][p:p + 8, :], st_q[u % 2])
            free["rh"] = free["rl"] = (m,)
            if g == 3:
                free[name] = (m,)
            proj[("unit", u)] = m
            yield

        def prepare(u):
            b, g = u // 4, u % 4
            if g == 0:
                yield from batch_projection(b)
            Q, K = Qp[u % 2], Kp[u % 2]
            fresh = unit_free[u % 2]
            yield from rope(u, g, "cq", "wqA", "wqB", qc, proj["qc"], Q, "hhl", fresh)
            if g == 3:
                free["qc"] = ((pe.sem, pe.n),)
            yield from rope(u, g, "ck", "wkA", "wkB", xnT, proj["x"], K, "hlh", fresh)
            if g == 3:
                free["xnT"] = ((pe.sem, pe.n),)
            pe.wait(proj[("unit", u)], m_mask, m_one)
            dve.wait(*free["mx"])
            for qt in range(8):
                n = 128 * (qt + 1)
                per = 2 if n <= 512 else 1
                for h in range(0, 4, per):
                    s = take_s()
                    for j in range(per):
                        lhs = Q[0:120, h + j, 128 * qt:128 * qt + 128]
                        for c in range(0, n, 512):
                            e = min(c + 512, n)
                            last = e == n
                            o = S[s][:, 512 * j + c:512 * j + e]
                            pe.do(te.matmul, o, lhs, K[0:120, h + j, c:e], start=True, stop=not last, inc=False)
                            if last:
                                m = pe.do(te.matmul, S[s][:, 512 * j + n - 128:512 * j + n], identb[:], mqkb[:],
                                          start=False, stop=True)
                    dve.wait(m)
                    if per == 2:
                        src = S[s][:].rearrange("p (j k) -> p j k", j=2)[:, :, 0:n]
                    else:
                        src = S[s][:, 0:n]
                    m = dve.do(ve.tensor_reduce, mx[:, qt, h:h + per], src, AX.X, ALU.max, negate=True)
                    s_free[s] = (m,)
                    yield
            s = take_s()
            pe.wait(m)
            for qt in range(8):
                m = pe.do(te.transpose, S[s][0:4, 128 * qt:128 * qt + 128], mx[:, qt, :], ident[:], inc=(qt == 7))
            free["mx"] = (m,)
            dve.wait(m, *free["mT"])
            m = dve.do(ve.tensor_copy, mT[:], S[s][0:4, :])
            s_free[s] = (m,)
            sp.wait(m)
            for h in range(4):
                m = sp.dma(ye.dma_start, Q[120:121, h, :].bitcast(F32), mT[h:h + 1, :].bitcast(F32), st_m[u % 2])
            free["mT"] = (m,)
            proj[("max", u)] = m
            yield

        def attend(u):
            b, g = u // 4, u % 4
            Q, K = Qp[u % 2], Kp[u % 2]
            V = V2[b % 2]
            pe.wait(proj[("max", u)], proj[("V", b)])
            pend = []

            def flush():
                kb, c, oa, tiles, first, last = pend.pop(0)
                for h in range(4):
                    i, ready = tiles[h // 2]
                    pe.wait(ready)
                    m = pe.do(te.matmul, A[oa][32 * h:32 * h + 32, c:512], V[:, kb, 4 * g + h, :], P[i][:, h % 2, c:512],
                              start=first, stop=last, tile_position=(0, 32 * h), inc=(h % 2 == 1))
                    if h % 2:
                        p_free[i] = (m,)
                return m

            for qh in range(2):
                oa = take_a()
                nb = 4 * qh + 4
                for kb in range(nb):
                    c = max(0, 128 * (kb - 4 * qh))
                    diag = kb >= 4 * qh
                    tiles = []
                    for hp in range(2):
                        s = take_s()
                        for j in range(2):
                            h = 2 * hp + j
                            pe.do(te.matmul, S[s][:, 512 * j + c:512 * j + 512], K[0:121, h, 128 * kb:128 * kb + 128],
                                  Q[0:121, h, 512 * qh + c:512 * qh + 512], start=True, stop=not diag, inc=False) if diag else None
                            if diag:
                                m = pe.do(te.matmul, S[s][:, 512 * j + c:512 * j + c + 128], identb[:], mkqb[:],
                                          start=False, stop=True, inc=(j == 1))
                            else:
                                m = pe.do(te.matmul, S[s][:, 512 * j:512 * j + 512], K[0:121, h, 128 * kb:128 * kb + 128],
                                          Q[0:121, h, 512 * qh:512 * qh + 512], start=True, stop=True, inc=(j == 1))
                        i = attend.k % NP
                        attend.k += 1
                        act.wait(m, *p_free[i])
                        m = act.do(se.activation, P[i][:, :, c:512],
                                   S[s][:].rearrange("p (j k) -> p j k", j=2)[:, :, c:512], ACT.Exp, scale=float(1.0 / np.sqrt(np.float32(40.0))))
                        s_free[s] = (m,)
                        tiles.append((i, m))
                        if hp == 0 and pend:
                            flush()
                    pend.append((kb, c, oa, tiles, kb == 0, kb == nb - 1))
                    yield
                m = flush()
                dve.wait(m, *free["oT"])
                m = dve.do(ve.tensor_copy, oT[:], A[oa][:])
                a_free[oa] = (m,)
                s = take_s()
                pe.wait(m)
                for i in range(4):
                    m = pe.do(te.transpose, S[s][:, 128 * i:128 * i + 128], oT[:, 128 * i:128 * i + 128], ident[:], inc=(i == 3))
                free["oT"] = (m,)
                o = S[s][:, 0:512].rearrange("p (n h d) -> p n h d", n=4, h=4)
                dve.wait(m)
                m = dve.do(ve.reciprocal, rec[:, :, :, None], o[:, :, :, 8:9])
                dve.wait(m, *free["at"])
                m = dve.do(ve.tensor_tensor, at[:, 4 * qh:4 * qh + 4, 32 * g:32 * g + 32].rearrange("p n (h d) -> p n h d", h=4),
                           o[:, :, :, 0:8], rec[:, :, :, None].broadcast_to([128, 4, 4, 8]), ALU.mult)
                s_free[s] = (m,)
                yield
            unit_free[u % 2] = ((pe.sem, pe.n),)
            if g == 3:
                v_free[b % 2] = ((pe.sem, pe.n),)
                m_at = m
                for k in range(2):
                    m = transposed(at[:, 4 * k:4 * k + 4, :], aT, 4, m_at, free["aT"])
                    s = take_s()
                    pe.wait(m)
                    for i in range(4):
                        m = pe.do(te.matmul, S[s][:, 128 * i:128 * i + 128], aT[:, 128 * i:128 * i + 128], W["wo0"][:],
                                  start=True, stop=True, inc=(i == 3))
                    free["aT"] = (m,)
                    dve.wait(m)
                    xb = x[:, 8 * b + 4 * k:8 * b + 4 * k + 4, :].rearrange("p n d -> p (n d)")
                    m_x = dve.do(ve.tensor_tensor, xb, xb, S[s][:, 0:512], ALU.add)
                    s_free[s] = (m_x,)
                free["at"] = (m,)
                m = m_x
                x_ready[b] = m
                yield

        attend.k = 0
        NU = 4 * B
        for _ in prepare(0):
            pass
        for u in range(NU):
            run_beside(attend(u), prepare(u + 1) if u + 1 < NU else iter(()), 0.40)
    barrier()

    if stop >= 1:
        ffn0(nc, ctx, locals())
    if stop >= 2:
        attn1(nc, ctx, locals())
    if stop >= 3:
        ffn1(nc, ctx, locals())

    sp.wait(*x_ready)
    st_o = stream("d_o")
    o_v = out.rearrange("(n p) d -> p n d", p=128)
    for b in range(B):
        m = sp.dma(ye.dma_start, o_v[:, 8 * b:8 * b + 8, :], x[:, 8 * b:8 * b + 8, :], st_o)
    sp.wait(m)

    with ctx:
        block = ctx.enter_context(nc.Block())

        @block.sync
        def _(eng):
            sp.play(eng)

        @block.gpsimd
        def _(eng):
            pool.play(eng)

        @block.scalar
        def _(eng):
            act.play(eng)

        @block.vector
        def _(eng):
            dve.play(eng)

        @block.tensor
        def _(eng):
            pe.play(eng)


def ffn0(nc, ctx, g):
    pe, dve, act, pool, sp = (g[k] for k in ("pe", "dve", "act", "pool", "sp"))
    te, ve, se, ge, ye = (g[k] for k in ("te", "ve", "se", "ge", "ye"))
    sb, S, A, take_s, take_a, s_free, a_free = (g[k] for k in ("sb", "S", "A", "take_s", "take_a", "s_free", "a_free"))
    x, x_ready, a, stream = g["x"], g["x_ready"], g["a"], g["stream"]
    with ExitStack() as ph:
        w1 = sb(ph, "w1", [128, 8, 1024])
        w2 = sb(ph, "w2", [128, 8, 4, 128])
        rw = sb(ph, "rw", [128, 8])
        rb = sb(ph, "rb", [128, 8])
        iota = sb(ph, "iota0", [128, 8])
        st_r, st_w = stream("d_r0"), [stream(f"d_w0{e}") for e in range(4)]
        sp.dma(ye.dma_start, rw[:], a["rw"], st_r)
        sp.dma(ye.dma_start, iota[:], a["iota"], st_r)
        m_rw = sp.dma(ye.dma_start, rb[:], a["rb"], st_r)
        m_w = {}
        for e in range(4):
            sp.dma(ye.dma_start, w1[:, 2 * e:2 * e + 2, :], a["w1"][:, 2 * e:2 * e + 2, :], st_w[e])
            m_w[e] = sp.dma(ye.dma_start, w2[:, 2 * e:2 * e + 2, :, :], a["w2"][:, 2 * e:2 * e + 2, :, :], st_w[e])
        xn = sb(ph, "xn0", [128, 4, 128])
        xT = [sb(ph, f"xT0{i}", [128, 512]) for i in range(2)]
        lg = sb(ph, "lg", [128, 4, 8])
        m8 = sb(ph, "m8", [128, 4, 8])
        i8 = sb(ph, "i8", [128, 4, 8], U32)
        fi = sb(ph, "fi", [128, 4])
        nm = sb(ph, "nm", [128, 4])
        ex = sb(ph, "ex", [128, 4, 8])
        sm = sb(ph, "sm", [128, 4])
        ws = [sb(ph, f"ws{i}", [128, 4, 8]) for i in range(2)]
        th = [sb(ph, f"th{i}", [128, 512]) for i in range(2)]
        uu = [sb(ph, f"uu{i}", [128, 512]) for i in range(2)]
        h = [sb(ph, f"h{i}", [128, 4, 512]) for i in range(2)]
        h_free, t_free = [(), ()], [(), ()]
        f = {"xn": (), "xT": [(), ()], "small": (), "ws": [(), ()]}

        def front(c):
            xc = x[:, 4 * c:4 * c + 4, :]
            m = g["layernorm"](xc, xn, 4, 1e-5, [x_ready[c // 2]], f["xn"])
            m_t = g["transposed"](xn, xT[c % 2], 4, m, f["xT"][c % 2])
            f["xn"] = (m_t,)
            s = take_s()
            pe.wait(m_t, m_rw)
            for i in range(4):
                m = pe.do(te.matmul, S[s][:, 8 * i:8 * i + 8], xT[c % 2][:, 128 * i:128 * i + 128], rw[:],
                          start=True, stop=True, inc=(i == 3))
            dve.wait(m, *f["small"])
            m = dve.do(ve.tensor_tensor, lg[:], S[s][:, 0:32].rearrange("p (n e) -> p n e", e=8),
                       rb[:, None, :].broadcast_to([128, 4, 8]), ALU.add)
            s_free[s] = (m,)
            dve.wait(m)
            for i in range(4):
                m = dve.do(ve.max, m8[:, i, :], lg[:, i, :])
            dve.wait(m)
            for i in range(4):
                m = dve.do(ve.max_index, i8[:, i, :], m8[:, i, :], lg[:, i, :])
            m_n = dve.do(ve.tensor_scalar, nm[:], m8[:, :, 0], -1.0, None, ALU.mult)
            dve.wait(m)
            m_i = dve.do(ve.tensor_copy, fi[:], i8[:, :, 0])
            act.wait(m_n)
            for i in range(4):
                m = act.do(se.activation, ex[:, i, :], lg[:, i, :], ACT.Exp, bias=nm[:, i:i + 1])
            dve.wait(m)
            m = dve.do(ve.tensor_reduce, sm[:], ex[:], AX.X, ALU.add)
            dve.wait(m)
            m = dve.do(ve.reciprocal, sm[:], sm[:])
            dve.wait(m, m_i, *f["ws"][c % 2])
            for i in range(4):
                m = dve.do(ve.tensor_scalar, ws[c % 2][:, i, :], iota[:], fi[:, i:i + 1], sm[:, i:i + 1], ALU.is_equal, ALU.mult)
            dve.wait(m)
            m = dve.do(ve.tensor_scalar, ws[c % 2][:], ws[c % 2][:], 0.5, None, ALU.mult)
            f["small"] = (m,)
            return m_t, m

        ready = front(0)
        pend = []

        def down():
            c, e, hb, m_h, m_ws = pend.pop(0)
            o = take_a()
            pe.wait(m_h)
            for i in range(4):
                for j in range(4):
                    m = pe.do(te.matmul, A[o][:, 128 * i:128 * i + 128], h[hb][:, j, 128 * i:128 * i + 128], w2[:, e, j, :],
                              start=(j == 0), stop=(j == 3), inc=(i == 3 and j == 3))
            h_free[hb] = (m,)
            dve.wait(m, m_ws, x_ready[c // 2])
            for i in range(4):
                xi = x[:, 4 * c + i, :]
                m = dve.do(ve.scalar_tensor_tensor, xi, A[o][:, 128 * i:128 * i + 128], ws[c % 2][:, i, e:e + 1], xi, ALU.mult, ALU.add)
            a_free[o] = (m,)
            x_ready[c // 2] = m
            f["ws"][c % 2] = (m,)

        k = 0
        for c in range(8):
            m_t, m_ws = ready
            for e in range(8):
                hb = (8 * c + e) % 2
                dve.wait(*h_free[hb])
                for j in range(4):
                    s = take_s()
                    pe.wait(m_t, m_w[e // 2])
                    pe.do(te.matmul, S[s][:, 0:512], w1[:, e, 128 * j:128 * j + 128], xT[c % 2][:], start=True, stop=True, inc=False)
                    m = pe.do(te.matmul, S[s][:, 512:1024], w1[:, e, 512 + 128 * j:640 + 128 * j], xT[c % 2][:], start=True, stop=True)
                    q = k % 2
                    k += 1
                    act.wait(m, *t_free[q])
                    m = act.do(se.activation, th[q][:], S[s][:, 0:512], ACT.Tanh, scale=0.5)
                    dve.wait(m)
                    m = dve.do(ve.scalar_tensor_tensor, uu[q][:], th[q][:], 1.0, S[s][:, 0:512], ALU.add, ALU.mult)
                    dve.wait(m)
                    m = dve.do(ve.tensor_tensor, h[hb][:, j, :], uu[q][:], S[s][:, 512:1024], ALU.mult)
                    t_free[q] = (m,)
                    s_free[s] = (m,)
                    if j == 1 and pend:
                        down()
                pend.append((c, e, hb, m, m_ws))
                if e == 7:
                    f["xT"][c % 2] = ((pe.sem, pe.n),)
                if e == 3 and c < 7:
                    ready = front(c + 1)
        down()
    g["barrier"]()


def attn1(nc, ctx, g):
    pe, dve, act, pool, sp = (g[k] for k in ("pe", "dve", "act", "pool", "sp"))
    te, ve, se, ge, ye = (g[k] for k in ("te", "ve", "se", "ge", "ye"))
    sb, S, A, take_s, take_a, s_free, a_free = (g[k] for k in ("sb", "S", "A", "take_s", "take_a", "s_free", "a_free"))
    x, x_ready, a, stream, ident = g["x"], g["x_ready"], g["a"], g["stream"], g["ident"]
    with ExitStack() as ph:
        st = stream("d_a1")
        wt = {n: sb(ph, n, [128, 128]) for n in ("uq", "uk", "uv", "ug", "uo")}
        bias = sb(ph, "bias1", [128, 4])
        bo = sb(ph, "bo", [128, 128])
        hm = sb(ph, "hm", [128, 16])
        tp = sb(ph, "tp", [128, 16, 384])
        for n in wt:
            sp.dma(ye.dma_start, wt[n][:], a[n], st)
        sp.dma(ye.dma_start, bias[:], a["bias1"], st)
        sp.dma(ye.dma_start, bo[:], a["bo"], st)
        m_w = sp.dma(ye.dma_start, hm[:], a["hm"], st)
        st_t = stream("d_tp")
        m_tp = sp.dma(ye.dma_start, tp[:], a["tp"], st_t)
        xn = sb(ph, "xn1", [128, 8, 128])
        xT = sb(ph, "xT1", [128, T])
        qT, kT, gT = (sb(ph, n, [128, T]) for n in ("qT", "kT", "gT"))
        V = sb(ph, "Va1", [128, 8, 16, 9])
        qm = sb(ph, "qm", [128, 16, T])
        NR = 4
        sc = [sb(ph, f"sc{i}", [128, 384]) for i in range(NR)]
        pr = [sb(ph, f"pr{i}", [128, 384]) for i in range(NR)]
        pt = [sb(ph, f"pt{i}", [128, 384]) for i in range(NR)]
        mx = [sb(ph, f"mxa{i}", [128, 1]) for i in range(NR)]
        nm = [sb(ph, f"nm1{i}", [128, 1]) for i in range(NR)]
        rec = sb(ph, "rec1", [128, 16])
        at = sb(ph, "at1", [128, 128])
        ga = sb(ph, "ga", [128, 128])
        m_v1 = pool.do(ge.memset, V[:, :, :, 8:9], 1.0)
        pool.wait(m_w)
        m_w = pool.do(ge.tensor_scalar, bias[:, 2:3], bias[:, 2:3], 0.5, 1.0, ALU.mult, ALU.mult)
        scale = float(8 ** -0.5)
        pt_free, at_free, ga_free = [()] * NR, (), ()
        k = 0
        for b in range(B):
            xb = x[:, 8 * b:8 * b + 8, :]
            m = g["layernorm"](xb, xn, 8, 1e-5, [x_ready[b]], ((pe.sem, pe.n),))
            m_t = g["transposed"](xn, xT, 8, m, ((pe.sem, pe.n),))
            mm = {}
            for n, w, dst, col, func in (("q", "uq", qT, 0, ACT.Identity), ("k", "uk", kT, 1, ACT.Identity), ("g", "ug", gT, 2, ACT.Tanh)):
                s = take_s()
                pe.wait(m_t, m_w)
                for i in range(2):
                    m = pe.do(te.matmul, S[s][:, 512 * i:512 * i + 512], wt[w][:], xT[:, 512 * i:512 * i + 512],
                              start=True, stop=True, inc=(i == 1))
                act.wait(m, (pe.sem, pe.n))
                m = act.do(se.activation, dst[:], S[s][:], func, bias=bias[:, col:col + 1], scale=0.5 if n == "g" else 1.0)
                s_free[s] = (m,)
                mm[n] = m
            dve.wait(mm["g"])
            m_g = dve.do(ve.tensor_scalar, gT[:], gT[:], 1.0, 0.5, ALU.add, ALU.mult)
            s = take_s()
            for i in range(8):
                m = pe.do(te.matmul, S[s][:, 128 * i:128 * i + 128], xT[:, 128 * i:128 * i + 128], wt["uv"][:],
                          start=True, stop=True, inc=(i == 7))
            dve.wait(m, m_v1, (pe.sem, pe.n))
            m_v = dve.do(ve.tensor_copy, V[:, :, :, 0:8], S[s][:].rearrange("p (n h d) -> p n h d", n=8, h=16))
            s_free[s] = (m_v,)
            pool.wait(mm["q"], m_w, (pe.sem, pe.n))
            m_qm = [pool.do(ge.tensor_scalar, qm[:, h, :], qT[:], hm[:, h:h + 1], scale, ALU.mult, ALU.mult) for h in range(16)]
            for qt in range(8):
                k0 = max(0, qt - 2)
                nk = 128 * (qt + 1 - k0)
                to = 384 - nk
                oa = take_a()
                stage = []

                def scores(h):
                    nonlocal k
                    s = take_s()
                    pe.wait(m_qm[h], mm["k"])
                    m = pe.do(te.matmul, S[s][:, 0:nk], qm[:, h, 128 * qt:128 * qt + 128], kT[:, 128 * k0:128 * k0 + nk], start=True, stop=True)
                    r = k % NR
                    k += 1
                    dve.wait(m, m_tp)
                    m = dve.do(ve.tensor_tensor_reduce, out=sc[r][:, 0:nk], in0=S[s][:, 0:nk], in1=tp[:, h, to:384], scale=1.0,
                               scalar=-3e38, op0=ALU.add, op1=ALU.max, accum_out=mx[r][:])
                    dve.wait(m)
                    m = dve.do(ve.tensor_scalar, nm[r][:], mx[r][:], -1.0, None, ALU.mult)
                    act.wait(m)
                    m = act.do(se.activation, pr[r][:, 0:nk], sc[r][:, 0:nk], ACT.Exp, bias=nm[r][:])
                    stage.append((h, r, s, m))

                def turn(h, r, s, m):
                    pe.wait(m)
                    for i in range(nk // 128):
                        m = pe.do(te.transpose, S[s][:, 512 + 128 * i:640 + 128 * i], pr[r][:, 128 * i:128 * i + 128], ident[:],
                                  inc=(i == nk // 128 - 1))
                    dve.wait(m, *pt_free[r])
                    m = dve.do(ve.tensor_copy, pt[r][:, 0:nk], S[s][:, 512:512 + nk])
                    s_free[s] = (m,)
                    return (h, r, m)

                def values(h, r, m):
                    pe.wait(m, m_v)
                    for i in range(nk // 128):
                        m = pe.do(te.matmul, A[oa][:, 16 * h:16 * h + 9], pt[r][:, 128 * i:128 * i + 128], V[:, k0 + i, h, :],
                                  start=(i == 0), stop=(i == nk // 128 - 1), inc=(i == nk // 128 - 1))
                    pt_free[r] = (m,)
                    return m

                late = []
                for h in range(16):
                    scores(h)
                    if len(stage) == 2:
                        late.append(turn(*stage.pop(0)))
                    if len(late) == 2:
                        m = values(*late.pop(0))
                while stage:
                    late.append(turn(*stage.pop(0)))
                while late:
                    m = values(*late.pop(0))
                o = A[oa][:, 0:256].rearrange("p (h d) -> p h d", d=16)
                dve.wait(m)
                m = dve.do(ve.reciprocal, rec[:, :, None], o[:, :, 8:9])
                dve.wait(m, *at_free)
                m = dve.do(ve.tensor_tensor, at[:].rearrange("p (h d) -> p h d", d=8), o[:, :, 0:8],
                           rec[:, :, None].broadcast_to([128, 16, 8]), ALU.mult)
                pe.wait(m)
                m = pe.do(te.transpose, A[oa][:, 256:384], at[:], ident[:])
                at_free = (m,)
                dve.wait(m, m_g, *ga_free)
                m = dve.do(ve.scalar_tensor_tensor, ga[:], A[oa][:, 256:384], bias[:, 3:4], gT[:, 128 * qt:128 * qt + 128], ALU.add, ALU.mult)
                pe.wait(m)
                m = pe.do(te.matmul, A[oa][:, 384:512], ga[:], wt["uo"][:], start=True, stop=True)
                ga_free = (m,)
                dve.wait(m)
                xi = x[:, 8 * b + qt, :]
                m = dve.do(ve.tensor_tensor, xi, xi, A[oa][:, 384:512], ALU.add)
                a_free[oa] = (m,)
                dve.wait(m)
                m = dve.do(ve.tensor_tensor, xi, xi, bo[:], ALU.add)
                x_ready[b] = m
    g["barrier"]()


def ffn1(nc, ctx, g):
    pe, dve, act, pool, sp = (g[k] for k in ("pe", "dve", "act", "pool", "sp"))
    te, ve, se, ge, ye = (g[k] for k in ("te", "ve", "se", "ge", "ye"))
    sb, S, A, take_s, take_a, s_free, a_free = (g[k] for k in ("sb", "S", "A", "take_s", "take_a", "s_free", "a_free"))
    x, x_ready, a, stream, ident = g["x"], g["x_ready"], g["a"], g["stream"], g["ident"]
    with ExitStack() as ph:
        st = stream("d_f1")
        aw = sb(ph, "aw", [128, 128])
        cols = sb(ph, "cols", [128, 3])
        gam, bet = sb(ph, "gam", [128, 128]), sb(ph, "bet", [128, 128])
        mw, mb = sb(ph, "mw", [128, 8]), sb(ph, "mb", [128, 8])
        e1 = sb(ph, "e1", [128, 8, 256])
        e2 = sb(ph, "e2", [128, 8, 2, 128])
        b1 = sb(ph, "b1", [128, 8, 2])
        b2 = sb(ph, "b2", [8, 128])
        gm = sb(ph, "gm", [128, 3, 128])
        gca, gcb = sb(ph, "gca", [128, 128]), sb(ph, "gcb", [128, 128])
        iota = sb(ph, "iota1", [128, 8])
        for n, t in (("aw", aw), ("cols", cols), ("gam", gam), ("bet", bet), ("mw", mw), ("mb", mb), ("e1", e1), ("e2", e2),
                     ("b1", b1), ("b2", b2), ("gm", gm), ("gca", gca), ("gcb", gcb), ("iota", iota)):
            m_w = sp.dma(ye.dma_start, t[:], a[n], st)

        SQ, DEG = 10, 9
        G, GT = sb(ph, "G", [128, 3, 128]), sb(ph, "GT", [128, 3, 128])
        F = [sb(ph, f"F{i}", [128, 3, 128]) for i in range(2)]
        FT = [sb(ph, f"FT{i}", [128, 3, 128]) for i in range(2)]
        R = sb(ph, "R", [128, 128])
        flat = lambda t: t[:].rearrange("p n d -> p (n d)")
        dve.wait(m_w)
        dve.do(ve.tensor_scalar, cols[:, 1:2], cols[:, 1:2], 0.5, None, ALU.mult)
        m = dve.do(ve.tensor_scalar, flat(G), flat(gm), float(2.0 ** -SQ), None, ALU.mult)

        def turned(src, dst, ready):
            s = take_s()
            pe.wait(ready)
            for i in range(3):
                m = pe.do(te.transpose, S[s][:, 128 * i:128 * i + 128], src[:, i, :], ident[:], inc=(i == 2))
            dve.wait(m)
            m = dve.do(ve.tensor_copy, flat(dst), S[s][:, 0:384])
            s_free[s] = (m,)
            return m

        m_gt = turned(G, GT, m)
        m = dve.do(ve.tensor_scalar, flat(F[0]), flat(G), 1.0 / DEG, None, ALU.mult)
        for d in range(DEG - 1, 0, -1):
            s = take_s()
            pe.wait(m, m_gt)
            for i in range(3):
                m = pe.do(te.matmul, S[s][:, 128 * i:128 * i + 128], GT[:, i, :], F[0][:, i, :], start=True, stop=True, inc=(i == 2))
            dve.wait(m)
            m = dve.do(ve.tensor_tensor, flat(F[0]), S[s][:, 0:384], flat(G), ALU.add)
            s_free[s] = (m,)
            if d > 1:
                dve.wait(m)
                m = dve.do(ve.tensor_scalar, flat(F[0]), flat(F[0]), 1.0 / d, None, ALU.mult)
        m = turned(F[0], FT[0], m)
        for n in range(SQ):
            f, ft, f2, ft2 = F[n % 2], FT[n % 2], F[1 - n % 2], FT[1 - n % 2]
            s = take_s()
            pe.wait(m)
            for i in range(3):
                pe.do(te.matmul, S[s][:, 128 * i:128 * i + 128], ft[:, i, :], f[:, i, :], start=True, stop=True, inc=False)
                m = pe.do(te.matmul, S[s][:, 512 + 128 * i:640 + 128 * i], f[:, i, :], ft[:, i, :], start=True, stop=True, inc=(i == 2))
            dve.wait(m)
            dve.do(ve.scalar_tensor_tensor, flat(f2), flat(f), 2.0, S[s][:, 0:384], ALU.mult, ALU.add)
            m = dve.do(ve.scalar_tensor_tensor, flat(ft2), flat(ft), 2.0, S[s][:, 512:896], ALU.mult, ALU.add)
            s_free[s] = (m,)
        f, ft = F[SQ % 2], FT[SQ % 2]
        dve.wait(m)
        for i in range(3):
            dve.do(ve.tensor_tensor, f[:, i, :], f[:, i, :], ident[:], ALU.add)
            m = dve.do(ve.tensor_tensor, ft[:, i, :], ft[:, i, :], ident[:], ALU.add)
        s = take_s()
        pe.wait(m)
        m = pe.do(te.matmul, S[s][:, 0:128], f[:, 1, :], ft[:, 0, :], start=True, stop=True)
        dve.wait(m)
        m = dve.do(ve.tensor_copy, G[:, 0, :], S[s][:, 0:128])
        pe.wait(m)
        m = pe.do(te.matmul, S[s][:, 512:640], G[:, 0, :], f[:, 2, :], start=True, stop=True)
        dve.wait(m)
        m_R = dve.do(ve.tensor_copy, R[:], S[s][:, 512:640])
        s_free[s] = (m_R,)

        n1 = [sb(ph, f"n1{i}", [128, 4, 128]) for i in range(2)]
        n2 = sb(ph, "n2", [128, 4, 128])
        nT = [sb(ph, f"nT{i}", [128, 512]) for i in range(2)]
        lg = sb(ph, "lg1", [128, 4, 8])
        m8 = sb(ph, "m81", [128, 4, 8])
        i8 = sb(ph, "i81", [128, 4, 8], U32)
        fi = sb(ph, "fi1", [128, 4, 2])
        dd = sb(ph, "dd", [128, 4])
        w01 = sb(ph, "w01", [128, 4, 2])
        wt2 = sb(ph, "wt2", [128, 8])
        wd = [sb(ph, f"wd{i}", [128, 4, 8]) for i in range(2)]
        wdT = sb(ph, "wdT", [8, 512])
        h = [sb(ph, f"h1{i}", [128, 2, 512]) for i in range(2)]
        acc = [sb(ph, f"acc{i}", [128, 4, 128]) for i in range(2)]
        ab = [sb(ph, f"ab{i}", [128, 512]) for i in range(2)]
        mo, mr, gt, df = (sb(ph, n, [128, 512]) for n in ("mo", "mr", "gt", "df"))
        h_free = [(), ()]
        pend = []

        def start_(c):
            p = c % 2
            xc = x[:, 4 * c:4 * c + 4, :]
            was = ((pe.sem, pe.n), (dve.sem, dve.n))
            m_n1 = g["layernorm"](xc, n1[p], 4, 1e-5, [x_ready[c // 2]], was)
            dve.wait(m_n1)
            m = g["layernorm"](n1[p], n2, 4, 1e-5, [m_n1], ())
            dve.wait(m)
            m = dve.do(ve.tensor_tensor, n2[:], n2[:], gam[:, None, :].broadcast_to([128, 4, 128]), ALU.mult)
            dve.wait(m)
            m = dve.do(ve.tensor_tensor, n2[:], n2[:], bet[:, None, :].broadcast_to([128, 4, 128]), ALU.add)
            m_t = g["transposed"](n2, nT[p], 4, m, was[:1])
            s = take_s()
            pe.wait(m_t)
            for i in range(4):
                m = pe.do(te.matmul, S[s][:, 8 * i:8 * i + 8], nT[p][:, 128 * i:128 * i + 128], mw[:],
                          start=True, stop=True, inc=False)
            m = pe.do(te.matmul, S[s][:, 512:1024], aw[:], nT[p][:], start=True, stop=True)
            act.wait(m, *was)
            m_ab = act.do(se.activation, ab[p][:], S[s][:, 512:1024], ACT.Gelu, bias=cols[:, 0:1])
            dve.wait(m)
            m = dve.do(ve.tensor_tensor, lg[:], S[s][:, 0:32].rearrange("p (n e) -> p n e", e=8),
                       mb[:, None, :].broadcast_to([128, 4, 8]), ALU.add)
            s_free[s] = (m, m_ab)
            dve.wait(m)
            for i in range(4):
                m = dve.do(ve.max, m8[:, i, :], lg[:, i, :])
            dve.wait(m)
            for i in range(4):
                m_i = dve.do(ve.max_index, i8[:, i, :], m8[:, i, :], lg[:, i, :])
            m = dve.do(ve.tensor_tensor, dd[:], m8[:, :, 0], m8[:, :, 1], ALU.subtract)
            dve.wait(m_i)
            m_i = dve.do(ve.tensor_copy, fi[:], i8[:, :, 0:2])
            act.wait(m)
            m = act.do(se.activation, dd[:], dd[:], ACT.Tanh, scale=0.5)
            dve.wait(m)
            m = dve.do(ve.tensor_scalar, w01[:, :, 0], dd[:], 0.5, 0.5, ALU.mult, ALU.add)
            m = dve.do(ve.tensor_scalar, w01[:, :, 1], dd[:], -0.5, 0.5, ALU.mult, ALU.add)
            dve.wait(m, m_i)
            for i in range(4):
                m = dve.do(ve.tensor_scalar, wt2[:], iota[:], fi[:, i, 0:1], w01[:, i, 0:1], ALU.is_equal, ALU.mult)
                m_2 = dve.do(ve.tensor_scalar, wd[p][:, i, :], iota[:], fi[:, i, 1:2], w01[:, i, 1:2], ALU.is_equal, ALU.mult)
                dve.wait(m_2)
                m = dve.do(ve.tensor_tensor, wd[p][:, i, :], wd[p][:, i, :], wt2[:], ALU.add)
                dve.wait(m)
            s = take_s()
            pe.wait(m)
            for i in range(4):
                m = pe.do(te.transpose, S[s][0:8, 128 * i:128 * i + 128], wd[p][:, i, :], ident[:], inc=(i == 3))
            dve.wait(m)
            m = dve.do(ve.tensor_copy, wdT[:], S[s][0:8, 0:512])
            pe.wait(m)
            for i in range(4):
                m = pe.do(te.matmul, S[s][:, 512 + 128 * i:640 + 128 * i], wdT[:, 128 * i:128 * i + 128], b2[:], start=True, stop=True, inc=(i == 3))
            dve.wait(m)
            m = dve.do(ve.tensor_copy, flat(acc[p]), S[s][:, 512:1024])
            s_free[s] = (m,)
            return m_t, m_ab, m

        def down():
            c, e, hb, m_h = pend.pop(0)
            p = c % 2
            o = take_a()
            pe.wait(m_h)
            for i in range(4):
                for j in range(2):
                    m = pe.do(te.matmul, A[o][:, 128 * i:128 * i + 128], h[hb][:, j, 128 * i:128 * i + 128], e2[:, e, j, :],
                              start=(j == 0), stop=(j == 1), inc=(i == 3 and j == 1))
            h_free[hb] = (m,)
            dve.wait(m, (dve.sem, dve.n))
            for i in range(4):
                ai = acc[p][:, i, :]
                m = dve.do(ve.scalar_tensor_tensor, ai, A[o][:, 128 * i:128 * i + 128], wd[p][:, i, e:e + 1], ai, ALU.mult, ALU.add)
            a_free[o] = (m,)
            return m

        def finish(c, m_acc, m_ab):
            p = c % 2
            s = take_s()
            pe.wait(m_acc, m_R)
            for i in range(4):
                m = pe.do(te.transpose, S[s][:, 128 * i:128 * i + 128], acc[p][:, i, :], ident[:], inc=(i == 3))
            dve.wait(m)
            m = dve.do(ve.tensor_copy, mo[:], S[s][:, 0:512])
            pe.wait(m)
            m = pe.do(te.matmul, S[s][:, 512:1024], R[:], mo[:], start=True, stop=True)
            dve.wait(m)
            m = dve.do(ve.tensor_copy, mr[:], S[s][:, 512:1024])
            s_free[s] = (m,)
            s = take_s()
            pe.wait(m, m_ab)
            pe.do(te.matmul, S[s][:, 0:512], gca[:], ab[p][:], start=True, stop=False, inc=False)
            m_g = pe.do(te.matmul, S[s][:, 0:512], gcb[:], mr[:], start=False, stop=True)
            dve.wait(m)
            m_d = dve.do(ve.tensor_tensor, df[:], mr[:], ab[p][:], ALU.subtract)
            act.wait(m_g)
            m = act.do(se.activation, gt[:], S[s][:, 0:512], ACT.Tanh, bias=cols[:, 1:2], scale=0.5)
            dve.wait(m, m_d)
            m = dve.do(ve.scalar_tensor_tensor, df[:], gt[:], 1.0, df[:], ALU.add, ALU.mult)
            dve.wait(m)
            m = dve.do(ve.scalar_tensor_tensor, df[:], df[:], 0.5, ab[p][:], ALU.mult, ALU.add)
            pe.wait(m)
            for i in range(4):
                m = pe.do(te.transpose, S[s][:, 512 + 128 * i:640 + 128 * i], df[:, 128 * i:128 * i + 128], ident[:], inc=(i == 3))
            xc = x[:, 4 * c:4 * c + 4, :].rearrange("p n d -> p (n d)")
            m_1 = dve.do(ve.tensor_tensor, xc, xc, flat(n1[p]), ALU.add)
            dve.wait(m, m_1)
            m = dve.do(ve.tensor_tensor, xc, xc, S[s][:, 512:1024], ALU.add)
            s_free[s] = (m,)
            return m

        x_out = []
        ready = start_(0)
        for c in range(8):
            m_t, m_ab, m_a = ready
            for e in range(8):
                hb = e % 2
                s = take_s()
                pe.wait(m_t)
                for j in range(2):
                    m = pe.do(te.matmul, S[s][:, 512 * j:512 * j + 512], e1[:, e, 128 * j:128 * j + 128], nT[c % 2][:],
                              start=True, stop=True, inc=(j == 1))
                act.wait(m, *h_free[hb])
                for j in range(2):
                    m = act.do(se.activation, h[hb][:, j, :], S[s][:, 512 * j:512 * j + 512], ACT.Gelu, bias=b1[:, e, j:j + 1])
                s_free[s] = (m,)
                if pend:
                    down()
                pend.append((c, e, hb, m))
            m = down()
            if c < 7:
                ready = start_(c + 1)
            x_out.append(finish(c, m, m_ab))
        for b in range(B):
            x_ready[b] = x_out[2 * b + 1]


def constants():
    inv = 1.0 / 10000.0 ** (np.arange(0, 32, 2, dtype=np.float32) / 32)
    f = np.outer(np.arange(T, dtype=np.float32), inv)
    emb = np.concatenate([f, f], -1)
    c, s = np.cos(emb).T.astype(np.float32), np.sin(emb).T.astype(np.float32)
    s = np.concatenate([-s[:16], s[16:]], 0)
    k = np.arange(128)
    return {
        "ident": np.eye(128, dtype=np.float32),
        "cos": np.ascontiguousarray(np.tile(c, (4, 1))),
        "sin": np.ascontiguousarray(np.tile(s, (4, 1))),
        "iota": np.tile(np.arange(8, dtype=np.float32), (128, 1)),
        "hm": np.repeat(np.eye(16, dtype=np.float32), 8, axis=0),
        "mkq": np.where(k[:, None] > k[None, :], NEG, 0.0).astype(np.float32),
        "mqk": np.where(k[None, :] > k[:, None], NEG, 0.0).astype(np.float32),
    }


def rows(w, n=128):
    out = np.zeros((n,) + w.shape[1:], w.dtype)
    out[:w.shape[0]] = w
    return out


def spread(v):
    return np.broadcast_to(v[None, :], (128, v.shape[0]))


def rotated(w):
    r = w.reshape(w.shape[0], 16, 2, 16)
    return np.ascontiguousarray(r[:, :, ::-1, :]).reshape(w.shape)


def layout(i):
    wq = np.zeros((128, 128), np.float32)
    wq[:, :64] = i["L0_attn_W_q"]
    d = dict(constants())
    d.update({
        "x": i["L0_attn_x"].reshape(B * T, D),
        "wq": wq,
        "wqd": rows(i["L0_attn_W_qdec"]),
        "wkd": rows(i["L0_attn_W_kdec"]),
        "wvd": rows(i["L0_attn_W_vdec"]),
        "wo0": i["L0_attn_W_o"],
        "wkv": i["L0_attn_W_kv"],
        "gkv": rows(i["L0_attn_g_kv"].reshape(32, 1)),
        "wqA": rows(i["L0_attn_W_qrope"]),
        "wqB": rows(rotated(i["L0_attn_W_qrope"])),
        "wkA": i["L0_attn_W_krope"],
        "wkB": rotated(i["L0_attn_W_krope"]),
    })
    w = i["L1_attn_Wqkv"]
    bq = i["L1_attn_bqkv"].reshape(3, 128)
    bg = i["L1_attn_bgate"]
    ext = np.full((16, 640), NEG, np.float32)
    ext[:, [o + 127 for o in OFFS]] = i["L1_attn_pos_bias"].T
    p = np.arange(128)[:, None]
    j = np.arange(384)[None, :]
    d.update({
        "rw": i["L0_ffn_router_w"],
        "rb": spread(i["L0_ffn_router_b"]),
        "w1": i["L0_ffn_w1"].transpose(1, 0, 2),
        "w2": i["L0_ffn_w2"].reshape(8, 4, 128, 128).transpose(2, 0, 1, 3),
        "uq": w[0:128].T, "uk": w[128:256].T, "uv": w[256:384].T,
        "ug": i["L1_attn_Wgate"].T, "uo": i["L1_attn_Wout"].T,
        "bias1": np.stack([bq[0], bq[1], bg, bq[2]], 1),
        "bo": spread(i["L1_attn_bout"]),
        "tp": ext[:, p - j + 256 + 127].transpose(1, 0, 2),
        "aw": i["L1_ffn_abel_w"],
        "cols": np.stack([i["L1_ffn_abel_b"], np.broadcast_to(i["L1_ffn_gc_b"], (128,)), i["L1_ffn_abel_b"]], 1),
        "gam": spread(i["L1_ffn_ln_gamma"]), "bet": spread(i["L1_ffn_ln_beta"]),
        "mw": i["L1_ffn_moe_gate_w"], "mb": spread(i["L1_ffn_moe_gate_b"]),
        "e1": i["L1_ffn_ew1"].transpose(1, 0, 2),
        "e2": i["L1_ffn_ew2"].reshape(8, 2, 128, 128).transpose(2, 0, 1, 3),
        "b1": i["L1_ffn_eb1"].reshape(8, 2, 128).transpose(2, 0, 1),
        "b2": i["L1_ffn_eb2"],
        "gm": i["L1_ffn_gens"].transpose(1, 0, 2),
        "gca": np.broadcast_to(i["L1_ffn_gc_w"][0:128], (128, 128)),
        "gcb": np.broadcast_to(i["L1_ffn_gc_w"][128:256], (128, 128)),
    })
    return d


STOP = 9


def kernel(**inputs):
    import concourse.bacc as bacc
    from concourse.bass_utils import run_bass_kernel_spmd as run

    i = {k: np.asarray(v) for k, v in inputs.items()}
    nc = bacc.Bacc("TRN2", target_bir_lowering=False, num_devices=1)
    arrays = {"in_" + k: np.ascontiguousarray(v) for k, v in layout(i).items()}
    aps = {k[3:]: nc.dram_tensor(k, v.shape, mybir.dt.from_np(v.dtype), kind="ExternalInput").ap() for k, v in arrays.items()}
    out = nc.dram_tensor("out", (B * T, D), F32, kind="ExternalOutput").ap()
    program(nc, aps, out, STOP)
    r = run(nc, [arrays], core_ids=[0])
    return r.results[0]["out"].reshape(B, T, D)
```

```python
import numpy as np
import concourse.bass as bass
from concourse import mybir
from contextlib import ExitStack

F32 = mybir.dt.float32
F32R = mybir.dt.float32r
BF16 = mybir.dt.bfloat16
U32 = mybir.dt.uint32
ALU = mybir.AluOpType
ACT = mybir.ActivationFunctionType
AX = mybir.AxisListType

LAG = 4
SCALE1 = -float(8 ** -0.5)
PACE1 = [(2, 1.0), (0, 1.3)]
EVAC = 3
PACEF = [(1, 0.4), (1, 0.55)]
EXP = 12
LAG1 = 3
LAG2 = 4
NS = 3
NT3 = 5
NP = 5
PACE = [(0, 0.5), (0, 0.55)]
B, T, D = 4, 1024, 128
NT = B * T // 128
OFFS = sorted(set(range(33)) | {48, 64, 96, 128, 192})
NEG = -1.0e30
DA, DD = 3, 4
NE = NT + 7


class Queue:

    def __init__(self, sem, one_by_one=False):
        self.sem, self.ops, self.n, self.waited = sem, [], 0, {}
        self.one_by_one = one_by_one

    def wait(self, *marks):
        for m in marks:
            if m is not None and self.waited.get(m[0].name, 0) < m[1]:
                self.waited[m[0].name] = m[1]
                self.ops.append((None, m, None))

    def do(self, fn, *args, inc=True, **kw):
        if self.one_by_one and self.n:
            self.wait((self.sem, self.n))
        self.ops.append((fn, args, kw, (self.sem, 1) if inc else None))
        self.n += inc
        return (self.sem, self.n)

    def dma(self, fn, dst, src, stream):
        stream[1] += 16
        self.ops.append((fn, (dst, src), {}, (stream[0], 16)))
        return (stream[0], stream[1])

    def indirect(self, fn, dst, dst_at, src, src_at, stream):
        stream[1] += 16
        self.ops.append((fn, (dst, dst_at, src, src_at), {}, (stream[0], 16)))
        return (stream[0], stream[1])

    def play(self, eng):
        for op in self.ops:
            if op[0] is None:
                eng.wait_ge(op[1][0], op[1][1])
            else:
                ins = op[0](*op[1], **op[2])
                if op[3]:
                    ins.then_inc(*op[3])


def run_beside(main, side, late, ratio):
    k = -float(late)
    alive = True
    for _ in main:
        k += 1.0
        while alive and k >= ratio:
            k -= ratio
            try:
                next(side)
            except StopIteration:
                alive = False
    for _ in side:
        pass


def program(nc, a, out):
    ctx = ExitStack()

    def sem(name):
        return ctx.enter_context(nc.semaphore(name))

    pe, dve, act, pool, sp = (Queue(sem(n)) for n in ("s_pe", "s_dve", "s_act", "s_pool", "s_sp"))
    pool.one_by_one = True
    te, ve, se, ge, ye = nc.tensor, nc.vector, nc.scalar, nc.gpsimd, nc.sync

    def stream(name):
        return [sem(name), 0]

    def sb(st, name, shape, dt=F32):
        return st.enter_context(nc.sbuf_tensor(name, shape, dt))

    def barrier():
        last = [(q.sem, q.n) for q in (pe, dve, act, pool)]
        for q in (pe, dve, act, pool, sp):
            q.wait(*[m for m in last if m[1]])

    S = [ctx.enter_context(nc.psum_tensor(f"S{i}", [128, 1024], F32)) for i in range(3)]
    A = [ctx.enter_context(nc.psum_tensor(f"A{i}", [128, 512], F32)) for i in range(2)]
    s_free, a_free = [()] * 3, [()] * 2
    turn = {"s": 0, "a": 0}

    def take_s():
        i = turn["s"] % 3
        turn["s"] += 1
        pe.wait(*s_free[i])
        return i

    def take_a():
        i = turn["a"] % 2
        turn["a"] += 1
        pe.wait(*a_free[i])
        return i

    x = sb(ctx, "x", [128, NT, D])
    ident = sb(ctx, "ident", [128, 128])
    identb = sb(ctx, "identb", [128, 128], BF16)
    st_x = stream("d_x")
    st_c = stream("d_c")
    x_in = a["x"].rearrange("(n p) d -> p n d", p=128)
    x_done = [sp.dma(ye.dma_start, x[:, 8 * b:8 * b + 8, :], x_in[:, 8 * b:8 * b + 8, :], st_x) for b in range(1)]
    c_id = sp.dma(ye.dma_start, ident[:], a["ident"], stream("d_id"))
    dve.wait(c_id)
    m_idb = dve.do(ve.tensor_copy, identb[:], ident[:])
    x_ready = [x_done[0]] * B

    stats = sb(ctx, "stats", [128, 8, 6])
    mv = sb(ctx, "mv", [128, 8, 2])
    rs = sb(ctx, "rs", [128, 8])
    half = sb(ctx, "half", [128, 8])
    m_half = pool.do(ge.memset, half[:], -0.5)

    def rstd(var_ap, eps, n, ready):
        pool.wait(ready, m_half)
        m = pool.do(ge.tensor_scalar, rs[:, 0:n], var_ap, eps, 1.0, ALU.add, ALU.mult)
        pool.wait(m)
        return pool.do(ge.tensor_tensor, rs[:, 0:n], rs[:, 0:n], half[:, 0:n], ALU.pow)

    def layernorm_steps(src, dst, n, eps, ready, dst_free=()):
        dve.wait(*ready)
        for i in range(n):
            m = dve.do(ve.bn_stats, stats[:, i, :], src[:, i, :])
        yield
        dve.wait(m)
        for i in range(n):
            m = dve.do(ve.bn_aggr, mv[:, i, :], stats[:, i, :])
        r = rstd(mv[:, 0:n, 1], eps, n, m)
        yield
        for i in range(n):
            if i == 0:
                dve.wait(m, r, *dst_free)
            if i == 4:
                yield
            m = dve.do(ve.tensor_scalar, dst[:, i, :], src[:, i, :], mv[:, i, 0:1], rs[:, i:i + 1],
                       ALU.subtract, ALU.mult)
        return m

    def layernorm(*args):
        steps = layernorm_steps(*args)
        while True:
            try:
                next(steps)
            except StopIteration as end:
                return end.value

    def transposed(src, dst, n, ready, dst_free=()):
        s = take_s()
        pe.wait(ready, c_id)
        for i in range(n):
            m = pe.do(te.transpose, S[s][:, 128 * i:128 * i + 128], src[:, i, :], ident[:], inc=(i == n - 1))
        act.wait(m, *dst_free)
        m = act.do(se.activation, dst[:, 0:128 * n], S[s][:, 0:128 * n], ACT.Copy)
        s_free[s] = (m,)
        return m

    with ExitStack() as ph:
        t1, t2, t3 = (sb(ph, n, [128, 512]) for n in ("t1", "t2", "t3"))
        names = ("wq", "wqd", "wkd", "wvd", "wo0")
        W = {n: sb(ph, n, [128, 128]) for n in names}
        wkv = sb(ph, "wkv", [128, 32])
        gkv = sb(ph, "gkv", [128, 1])
        R = {n: sb(ph, n, [128, 512]) for n in ("wqA", "wqB", "wkA", "wkB")}
        cos, sin = sb(ph, "cos", [128, T]), sb(ph, "sin", [128, T])
        mkqb, mqkb = sb(ph, "mkqb", [128, 256], BF16), sb(ph, "mqkb", [128, 128], BF16)
        for n in names:
            sp.dma(ye.dma_start, W[n][:], a[n], st_c)
        for n in R:
            sp.dma(ye.dma_start, R[n][:], a[n], st_c)
        sp.dma(ye.dma_start, wkv[:], a["wkv"], st_c)
        sp.dma(ye.dma_start, gkv[:], a["gkv"], st_c)
        sp.dma(ye.dma_start, cos[:], a["cos"], st_c)
        sp.dma(ye.dma_start, sin[:], a["sin"], st_c)
        sp.dma(ye.dma_start, t1[:, 0:128], a["mkq"], st_c)
        w0 = sp.dma(ye.dma_start, t2[:, 0:128], a["mqk"], st_c)
        st_x2 = stream("d_x2")
        for b in range(1, B):
            m = sp.dma(ye.dma_start, x[:, 8 * b:8 * b + 8, :], x_in[:, 8 * b:8 * b + 8, :], st_x2)
        x_ready = [x_ready[0]] + [m] * (B - 1)

        xn = sb(ph, "xn", [128, 8, 128])
        xnT = sb(ph, "xnT", [128, T])
        qc = sb(ph, "qc", [128, T])
        kvs = sb(ph, "kvs", [128, 8, 32])
        kvT = sb(ph, "kvT", [128, T])
        CH = {n: sb(ph, n, [128, T], F32R) for n in ("cqh", "cql", "ckh", "ckl")}
        RH = {n: sb(ph, "r" + n, [128, T], F32R) for n in ("cqh", "cql", "ckh", "ckl")}
        Qp = [sb(ph, f"Qp{i}", [128, 2, T], F32R) for i in range(4)]
        Kp = [sb(ph, f"Kp{i}", [128, 2, T], F32R) for i in range(4)]
        V2 = [sb(ph, f"V{i}", [128, 8, 16, 9]) for i in range(2)]
        v_free = [(), ()]
        NP = 6
        P = [sb(ph, f"P{i}", [128, 2, 512]) for i in range(NP)]
        p_free = [()] * NP
        mx = sb(ph, "mx", [128, 8, 2])
        mT = sb(ph, "mT", [2, T], F32R)
        oT = sb(ph, "oT", [128, 512])
        rec = sb(ph, "rec", [128, 4, 2])
        osum = sb(ph, "osum", [128, 4, 2, 9])
        at = sb(ph, "at", [128, 8, 128])
        aT = sb(ph, "aT", [128, 512])

        dve.wait(w0)
        dve.do(ve.memset, mkqb[:, 0:128], NEG)
        dve.do(ve.tensor_copy, mkqb[:, 128:256], t1[:, 0:128])
        m_mask = dve.do(ve.tensor_copy, mqkb[:], t2[:, 0:128])
        dve.do(ve.tensor_scalar, W["wkd"][:], W["wkd"][:], gkv[:, 0:1], None, ALU.mult)
        m_w = dve.do(ve.tensor_scalar, W["wvd"][:], W["wvd"][:], gkv[:, 0:1], None, ALU.mult)
        m_z = pool.do(ge.memset, kvT[:], 0.0)
        for i in range(2):
            a_free[i] = (dve.do(ve.memset, A[i][:], 0.0),)
        for V in V2:
            m_v0 = pool.do(ge.memset, V[:, :, :, 8:9], 1.0)
        for i in range(4):
            m_one = pool.do(ge.memset, Kp[i][96:128, :, :].bitcast(F32), 1.0)

        st_q = [stream(f"d_q{i}") for i in range(4)]
        st_m = [stream(f"d_m{i}") for i in range(2)]
        free = {n: () for n in ("xnT", "qc", "kvT", "cq", "ck", "t1", "t2", "t3", "rcq", "rck", "mT", "oT", "osum", "at", "aT", "kvn", "xn", "mx")}
        unit_free = [()] * 4
        proj = {}

        def batch_projection(b):
            xb = x[:, 8 * b:8 * b + 8, :]
            m = yield from layernorm_steps(xb, xn, 8, 1e-5, [x_ready[b]], free["xn"])
            yield
            m_t = transposed(xn, xnT, 8, m, free["xnT"])
            free["xn"] = (m_t,)
            yield
            s = take_s()
            pe.wait(m_t, w0)
            for i in range(2):
                m = pe.do(te.matmul, S[s][:, 512 * i:512 * i + 512], W["wq"][:], xnT[:, 512 * i:512 * i + 512],
                          start=True, stop=True, inc=(i == 1))
            act.wait(m, *free["qc"])
            m_qc = act.do(se.activation, qc[:], S[s][:], ACT.Copy)
            s_free[s] = (m_qc,)
            yield
            s = take_s()
            for i in range(8):
                m = pe.do(te.matmul, S[s][:, 32 * i:32 * i + 32], xnT[:, 128 * i:128 * i + 128], wkv[:],
                          start=True, stop=True, inc=(i == 7))
            kv = S[s][:, 0:256].rearrange("p (n d) -> p n d", d=32)
            act.wait(m)
            m_sq = act.do(se.activation, kvs[:], kv, ACT.Square)
            dve.wait(m_sq)
            m = dve.do(ve.tensor_reduce, mv[:, :, 1], kvs[:], AX.X, ALU.add)
            pool.wait(m)
            m = pool.do(ge.tensor_scalar, mv[:, :, 1], mv[:, :, 1], 1.0 / 32, 1.0, ALU.mult, ALU.mult)
            m_r = rstd(mv[:, :, 1], 1e-6, 8, m)
            dve.wait(m_r)
            m_kv = dve.do(ve.tensor_tensor, kvs[:], kv, rs[:, :, None].broadcast_to([128, 8, 32]), ALU.mult)
            s_free[s] = (m_sq, m_kv)
            yield
            s = take_s()
            pe.wait(m_kv)
            for i in range(8):
                m = pe.do(te.transpose, S[s][0:32, 128 * i:128 * i + 128], kvs[:, i, :], ident[:], inc=(i == 7))
            act.wait(m, m_z, *free["kvT"])
            m_kvT = act.do(se.activation, kvT[0:32, :], S[s][0:32, :], ACT.Copy)
            s_free[s] = (m_kvT,)
            yield
            for n, w, src, ready in (("cq", "wqd", qc, m_qc), ("ck", "wkd", kvT, m_kvT)):
                s = take_s()
                pe.wait(ready, m_w)
                for i in range(2):
                    m = pe.do(te.matmul, S[s][:, 512 * i:512 * i + 512], W[w][:], src[:, 512 * i:512 * i + 512],
                              start=True, stop=True, inc=(i == 1))
                act.wait(m, *free[n])
                m_h = act.do(se.activation, CH[n + "h"][:], S[s][:], ACT.Copy)
                dve.wait(m_h, *free[n])
                m_l = dve.do(ve.tensor_tensor, CH[n + "l"][:], S[s][:], CH[n + "h"][:].bitcast(F32), ALU.subtract)
                s_free[s] = (m_h, m_l)
                proj[n] = (m_h, m_l)
                yield
            s = take_s()
            for i in range(8):
                m = pe.do(te.matmul, S[s][:, 128 * i:128 * i + 128], kvT[:, 128 * i:128 * i + 128], W["wvd"][:],
                          start=True, stop=True, inc=(i == 7))
            free["kvT"] = (m,)
            act.wait(m, m_v0, *v_free[b % 2])
            m_v = act.do(se.activation, V2[b % 2][:, :, :, 0:8],
                         S[s][:, :].rearrange("p (n h d) -> p n h d", n=8, h=16), ACT.Copy)
            s_free[s] = (m_v,)
            proj[("V", b)] = m_v
            proj["x"] = m_t
            proj["qc"] = m_qc
            yield

        def rope(g, name, wa, wb, src, ready):
            rh, rl = RH[name + "h"], RH[name + "l"]
            for i in range(2):
                c = slice(512 * i, 512 * i + 512)
                s = take_s()
                pe.wait(ready)
                pe.do(te.matmul, S[s][:, 0:512], R[wa][:, 128 * g:128 * g + 128], src[:, c], start=True, stop=True, inc=False)
                m = pe.do(te.matmul, S[s][:, 512:1024], R[wb][:, 128 * g:128 * g + 128], src[:, c], start=True, stop=True)
                dve.wait(m, *free["t1"], *free["t2"])
                m_1 = dve.do(ve.tensor_tensor, t1[:], S[s][:, 0:512], cos[:, c], ALU.mult)
                m_2 = dve.do(ve.tensor_tensor, t2[:], S[s][:, 512:1024], sin[:, c], ALU.mult)
                s_free[s] = (m_2,)
                pool.wait(m_2, *free["t3"])
                m_3 = pool.do(ge.tensor_tensor, t3[:], t1[:], t2[:], ALU.add)
                pool.wait(*free["r" + name])
                m_h = pool.do(ge.tensor_tensor, rh[:, c], t1[:], t2[:], ALU.add)
                free["t1"] = free["t2"] = (m_h,)
                m_l = pool.do(ge.tensor_tensor, rl[:, c], t3[:], rh[:, c].bitcast(F32), ALU.subtract)
                free["t3"] = (m_l,)
                yield
            proj["r" + name] = (m_h, m_l)

        def compute(n):
            b, g = n // 4, n % 4
            if g == 0:
                yield from batch_projection(b)
            yield from rope(g, "cq", "wqA", "wqB", qc, proj["qc"])
            yield from rope(g, "ck", "wkA", "wkB", xnT, proj["x"])
            if g == 3:
                free["qc"] = free["xnT"] = ((pe.sem, pe.n),)

        def ship(u):
            g, pair = u // 2 % 4, u % 2
            sp.wait(*unit_free[u % 4])
            for name, dst, order in (("cq", Qp[u % 4], "hhl"), ("ck", Kp[u % 4], "hlh")):
                sp.wait(*proj["r" + name], *proj[name])
                for h in range(2):
                    r, q = 32 * (2 * pair + h), 8 * (4 * g + 2 * pair + h)
                    for k, part in enumerate(order):
                        sp.dma(ye.dma_start, dst[32 * k:32 * k + 32, h, :].bitcast(F32),
                               RH[name + part][r:r + 32, :].bitcast(F32), st_q[u % 4])
                        m = sp.dma(ye.dma_start, dst[96 + 8 * k:104 + 8 * k, h, :].bitcast(F32),
                                   CH[name + part][q:q + 8, :].bitcast(F32), st_q[u % 4])
            proj[("unit", u)] = m
            if pair:
                both = (proj[("unit", u - 1)], m)
                free["rcq"] = free["rck"] = both
                if g == 3:
                    free["cq"] = free["ck"] = both

        def maxima(u):
            Q, K = Qp[u % 4], Kp[u % 4]
            pe.wait(m_mask, m_one, proj[("unit", u)])
            dve.wait(*free["mx"])
            for qt in range(8):
                n = 128 * (qt + 1)
                per = 2 if n <= 512 else 1
                for h in range(0, 2, per):
                    s = take_s()
                    for j in range(per):
                        lhs = Q[0:120, h + j, 128 * qt:128 * qt + 128]
                        for c in range(0, n, 512):
                            e = min(c + 512, n)
                            pe.do(te.matmul, S[s][:, 512 * j + c:512 * j + e], lhs, K[0:120, h + j, c:e],
                                  start=True, stop=e != n, inc=False)
                        m = pe.do(te.matmul, S[s][:, 512 * j + n - 128:512 * j + n], identb[:], mqkb[:],
                                  start=False, stop=True, inc=(j == per - 1))
                    dve.wait(m)
                    if per == 2:
                        src = S[s][:].rearrange("p (j k) -> p j k", j=2)[:, :, 0:n]
                    else:
                        src = S[s][:, 0:n]
                    m = dve.do(ve.tensor_reduce, mx[:, qt, h:h + per], src, AX.X, ALU.max, negate=True)
                    s_free[s] = (m,)
                    yield
            s = take_s()
            pe.wait(m)
            for qt in range(8):
                m = pe.do(te.transpose, S[s][0:2, 128 * qt:128 * qt + 128], mx[:, qt, :], ident[:], inc=(qt == 7))
            free["mx"] = (m,)
            dve.wait(m, *free["mT"])
            m = dve.do(ve.tensor_copy, mT[:], S[s][0:2, :])
            s_free[s] = (m,)
            pool.wait(m)
            for h in range(2):
                m = pool.dma(ge.dma_start, Q[120:121, h, :].bitcast(F32), mT[h:h + 1, :].bitcast(F32), st_m[u % 2])
            free["mT"] = (m,)
            proj[("max", u)] = m
            yield

        def attend(u):
            b, w = u // 8, u % 8
            Q, K = Qp[u % 4], Kp[u % 4]
            V = V2[b % 2]
            pe.wait(proj[("max", u)], proj[("V", b)])
            for qh in range(2):
                oa = take_a()
                nb = 4 * qh + 4
                for kb in range(nb):
                    c = max(0, 128 * (kb - 4 * qh))
                    diag = kb >= 4 * qh
                    wide = 128
                    if qh == 0 and kb == 1:
                        c, wide = 0, 256
                    s = take_s()
                    for h in range(2):
                        m = pe.do(te.matmul, S[s][:, 512 * h + c:512 * h + 512], K[0:121, h, 128 * kb:128 * kb + 128],
                                  Q[0:121, h, 512 * qh + c:512 * qh + 512], start=True, stop=not diag, inc=(h == 1 and not diag))
                        if diag:
                            m = pe.do(te.matmul, S[s][:, 512 * h + c:512 * h + c + wide], identb[:], mkqb[:, 256 - wide:256],
                                      start=False, stop=True, inc=(h == 1))
                    i = attend.k % NP
                    attend.k += 1
                    act.wait(m, *p_free[i])
                    m = act.do(se.activation, P[i][:, :, c:512], S[s][:].rearrange("p (j k) -> p j k", j=2)[:, :, c:512],
                               ACT.Exp, scale=float(1.0 / np.sqrt(np.float32(40.0))))
                    s_free[s] = (m,)
                    pend.append((u, qh, oa, kb, c, i, m))
                    if len(pend) == LAG:
                        flush()
                    if tails:
                        try:
                            next(tails[0])
                        except StopIteration:
                            tails.pop(0)
                    yield
            unit_free[u % 4] = ((pe.sem, pe.n),)

        pend, tails = [], []

        def flush():
            both = [pend.pop(0), pend.pop(0)]
            for e in both:
                pe.wait(e[6])
            for u, qh, oa, kb, c, i, _ in both:
                for h in range(2):
                    o = 64 * (kb % 2) + 32 * h
                    m = pe.do(te.matmul, A[oa][o:o + 9, c:512], V2[u // 8 % 2][:, kb, 2 * (u % 8) + h, :], P[i][:, h, c:512],
                              start=kb < 2, stop=kb >= 4 * qh + 2, tile_position=(0, o), inc=(h == 1))
                p_free[i] = (m,)
            if kb == 4 * qh + 3:
                if qh == 1 and u % 8 == 7:
                    v_free[u // 8 % 2] = (m,)
                tails.append(tail(u, qh, oa, m))

        def tail(u, qh, oa, ready):
            b, w = u // 8, u % 8
            act.wait(ready, *free["oT"])
            m = act.do(se.activation, oT[:], A[oa][:], ACT.Copy)
            a_free[oa] = (m,)
            yield
            s = take_s()
            pe.wait(m)
            for i in range(4):
                m = pe.do(te.transpose, S[s][:, 128 * i:128 * i + 128], oT[:, 128 * i:128 * i + 128], ident[:], inc=(i == 3))
            free["oT"] = (m,)
            o = S[s][:, 0:512].rearrange("p (n e h d) -> p n h d e", n=4, e=2, h=2)
            dve.wait(m, *free["osum"])
            for i in range(4):
                m = dve.do(ve.tensor_reduce, osum[:, i, :, :], o[:, i, :, 0:9, :], AX.X, ALU.add)
            s_free[s] = (m,)
            dve.wait(m)
            m = dve.do(ve.reciprocal, rec[:, :, :, None], osum[:, :, :, 8:9])
            dve.wait(m, *free["at"])
            m_at = dve.do(ve.tensor_tensor, at[:, 4 * qh:4 * qh + 4, 16 * w:16 * w + 16].rearrange("p n (h d) -> p n h d", h=2),
                          osum[:, :, :, 0:8], rec[:, :, :, None].broadcast_to([128, 4, 2, 8]), ALU.mult)
            free["osum"] = (m_at,)
            if w == 7 and qh == 1:
                for k in range(2):
                    yield
                    m = transposed(at[:, 4 * k:4 * k + 4, :], aT, 4, m_at, free["aT"])
                    yield
                    s = take_s()
                    pe.wait(m)
                    for i in range(4):
                        m = pe.do(te.matmul, S[s][:, 128 * i:128 * i + 128], aT[:, 128 * i:128 * i + 128], W["wo0"][:],
                                  start=True, stop=True, inc=(i == 3))
                    free["aT"] = (m,)
                    dve.wait(m)
                    xb = x[:, 8 * b + 4 * k:8 * b + 4 * k + 4, :].rearrange("p n d -> p (n d)")
                    x_ready[b] = dve.do(ve.tensor_tensor, xb, xb, S[s][:, 0:512], ALU.add)
                    s_free[s] = (x_ready[b],)
                free["at"] = (m,)

        attend.k = 0
        NU, NG = 8 * B, 4 * B

        def ahead(u):
            if u + 1 < NU:
                yield from maxima(u + 1)
            if u % 2 and u // 2 + 2 < NG:
                yield from compute(u // 2 + 2)

        def all_of(*parts):
            for part in parts:
                for _ in part:
                    pass

        all_of(compute(0))
        ship(0)
        ship(1)
        all_of(maxima(0), compute(1))
        for u in range(NU):
            if u % 2 == 0 and u + 2 < NU:
                ship(u + 2)
                ship(u + 3)
            run_beside(attend(u), ahead(u), *PACE[u % 2])
        while pend:
            flush()
        all_of(*tails)
    barrier()

    R = sb(ctx, "R", [128, 128])
    one = attn1_operands(nc, ctx, locals())
    rest = ffn0(nc, ctx, locals())
    attn1(nc, ctx, locals())
    one["stack"].close()
    ffn1(nc, ctx, locals())

    sp.wait(*x_ready)
    st_o = stream("d_o")
    o_v = out.rearrange("(n p) d -> p n d", p=128)
    for b in range(B):
        m = sp.dma(ye.dma_start, o_v[:, 8 * b:8 * b + 8, :], x[:, 8 * b:8 * b + 8, :], st_o)
    sp.wait(m)

    with ctx:
        block = ctx.enter_context(nc.Block())

        @block.sync
        def _(eng):
            sp.play(eng)

        @block.gpsimd
        def _(eng):
            pool.play(eng)

        @block.scalar
        def _(eng):
            act.play(eng)

        @block.vector
        def _(eng):
            dve.play(eng)

        @block.tensor
        def _(eng):
            pe.play(eng)


def attn1_operands(nc, ctx, g):
    dve, pool, sp, ge, ye, sb, a, stream = (g[k] for k in ("dve", "pool", "sp", "ge", "ye", "sb", "a", "stream"))
    ph = ExitStack()
    st = stream("d_a1")
    wt = {n: sb(ph, n, [128, 128]) for n in ("uv", "ug", "uo")}
    w3 = {n: sb(ph, n, [128, 4, 96]) for n in ("uq3", "uk3")}
    bias = sb(ph, "bias1", [128, 2])
    b3 = {n: sb(ph, n, [96, 4]) for n in ("bq3", "bk3")}
    m3 = {n: sb(ph, n, [96, 1]) for n in ("mq3", "mk3")}
    bo = sb(ph, "bo", [128, 128])
    tp = sb(ph, "tp", [128, 16, 320])
    share, posi, yg = sb(ph, "share", [128, 32]), sb(ph, "posi", [128, 32], U32), sb(ph, "yg", [128, 8, 128])
    o = dict(stack=ph, wt=wt, w3=w3, bias=bias, b3=b3, m3=m3, bo=bo, tp=tp, share=share, posi=posi, yg=yg)

    def load():
        for d in (wt, w3, b3, m3):
            for n in d:
                sp.dma(ye.dma_start, d[n][:], a[n], st)
        sp.dma(ye.dma_start, bias[:], a["bias1"], st)
        m_w = sp.dma(ye.dma_start, bo[:], a["bo"], st)
        m_tp = sp.dma(ye.dma_start, tp[:], a["tp"], stream("d_tp"))
        o["m_w"], o["m_tp"] = m_w, m_tp

    def prepare():
        m_tp = o["m_tp"]
        pool.wait(o["m_w"])
        pool.do(ge.tensor_scalar, bias[:, 0:1], bias[:, 0:1], 0.5, 1.0, ALU.mult, ALU.mult)
        m_b = pool.do(ge.tensor_scalar, b3["bq3"][:], b3["bq3"][:], SCALE1, 1.0, ALU.mult, ALU.mult)
        pool.wait(m_tp)
        for h in range(0, 16, 4):
            m_tp = pool.do(ge.tensor_scalar, tp[:, h:h + 4, :], tp[:, h:h + 4, :], -1.0, 1.0, ALU.mult, ALU.mult)
        o["m_b"], o["m_tp"] = m_b, m_tp

    o["load"], o["prepare"] = load, prepare
    return o


def exponentials(nc, ph, g):
    pe, dve, sp, te, ve, ye = (g[k] for k in ("pe", "dve", "sp", "te", "ve", "ye"))
    sb, S, take_s, s_free, a, stream, ident, R = (g[k] for k in ("sb", "S", "take_s", "s_free", "a", "stream", "ident", "R"))
    SQ, DEG = 10, 9
    gm = sb(ph, "gm", [128, 3, 128])
    m_w = sp.dma(ye.dma_start, gm[:], a["gm"], stream("d_gm"))
    G, GT = sb(ph, "G", [128, 3, 128]), sb(ph, "GT", [128, 3, 128])
    F = [sb(ph, f"F{i}", [128, 3, 128]) for i in range(2)]
    FT = [sb(ph, f"FT{i}", [128, 3, 128]) for i in range(2)]
    flat = lambda t: t[:].rearrange("p n d -> p (n d)")

    def turned(src, dst, ready):
        s = take_s()
        pe.wait(ready)
        for i in range(3):
            m = pe.do(te.transpose, S[s][:, 128 * i:128 * i + 128], src[:, i, :], ident[:], inc=(i == 2))
        dve.wait(m)
        m = dve.do(ve.tensor_copy, flat(dst), S[s][:, 0:384])
        s_free[s] = (m,)
        return m

    def steps():
        dve.wait(m_w)
        m = dve.do(ve.tensor_scalar, flat(G), flat(gm), float(2.0 ** -SQ), None, ALU.mult)
        m_gt = turned(G, GT, m)
        m = dve.do(ve.tensor_scalar, flat(F[0]), flat(G), 1.0 / DEG, None, ALU.mult)
        for d in range(DEG - 1, 0, -1):
            s = take_s()
            pe.wait(m, m_gt)
            for i in range(3):
                m = pe.do(te.matmul, S[s][:, 128 * i:128 * i + 128], GT[:, i, :], F[0][:, i, :], start=True, stop=True, inc=(i == 2))
            dve.wait(m)
            m = dve.do(ve.tensor_tensor, flat(F[0]), S[s][:, 0:384], flat(G), ALU.add)
            s_free[s] = (m,)
            if d > 1:
                dve.wait(m)
                m = dve.do(ve.tensor_scalar, flat(F[0]), flat(F[0]), 1.0 / d, None, ALU.mult)
            yield
        m = turned(F[0], FT[0], m)
        for n in range(SQ):
            f, ft, f2, ft2 = F[n % 2], FT[n % 2], F[1 - n % 2], FT[1 - n % 2]
            s = take_s()
            pe.wait(m)
            for i in range(3):
                pe.do(te.matmul, S[s][:, 128 * i:128 * i + 128], ft[:, i, :], f[:, i, :], start=True, stop=True, inc=False)
                m = pe.do(te.matmul, S[s][:, 512 + 128 * i:640 + 128 * i], f[:, i, :], ft[:, i, :], start=True, stop=True, inc=(i == 2))
            dve.wait(m)
            dve.do(ve.scalar_tensor_tensor, flat(f2), flat(f), 2.0, S[s][:, 0:384], ALU.mult, ALU.add)
            m = dve.do(ve.scalar_tensor_tensor, flat(ft2), flat(ft), 2.0, S[s][:, 512:896], ALU.mult, ALU.add)
            s_free[s] = (m,)
            yield
        f, ft = F[SQ % 2], FT[SQ % 2]
        dve.wait(m)
        for i in range(3):
            dve.do(ve.tensor_tensor, f[:, i, :], f[:, i, :], ident[:], ALU.add)
            m = dve.do(ve.tensor_tensor, ft[:, i, :], ft[:, i, :], ident[:], ALU.add)
        s = take_s()
        pe.wait(m)
        m = pe.do(te.matmul, S[s][:, 0:128], f[:, 1, :], ft[:, 0, :], start=True, stop=True)
        dve.wait(m)
        m = dve.do(ve.tensor_copy, G[:, 0, :], S[s][:, 0:128])
        pe.wait(m)
        m = pe.do(te.matmul, S[s][:, 512:640], G[:, 0, :], f[:, 2, :], start=True, stop=True)
        dve.wait(m)
        m_R = dve.do(ve.tensor_copy, R[:], S[s][:, 512:640])
        s_free[s] = (m_R,)

    return steps()


def ffn0(nc, ctx, g):
    pe, dve, act, pool, sp = (g[k] for k in ("pe", "dve", "act", "pool", "sp"))
    te, ve, se, ge, ye = (g[k] for k in ("te", "ve", "se", "ge", "ye"))
    sb, S, A, take_s, take_a, s_free, a_free = (g[k] for k in ("sb", "S", "A", "take_s", "take_a", "s_free", "a_free"))
    x, x_ready, a, stream, ident, one = (g[k] for k in ("x", "x_ready", "a", "stream", "ident", "one"))
    xs = nc.dram_tensor("xs", (NE * 128, 128), F32, kind="Internal").ap()
    ys = nc.dram_tensor("ys", (NE * 128, 128), F32, kind="Internal").ap()
    with ExitStack() as ph:
        w1 = sb(ph, "w1", [128, 8 * 1024])
        w2 = sb(ph, "w2", [128, 8 * 512])
        small = {n: sb(ph, n + "0", [128, w]) for n, w in
                 (("rw", 8), ("iota", 8), ("rb", 8), ("tri", 128), ("one", 128), ("thr", 256), ("upto", 64), ("tix", 7 * NE))}
        rw, iota, rb = small["rw"], small["iota"], small["rb"]
        zero = sb(ph, "zero0", [128, 128])
        st_r, st_w = stream("d_r0"), [stream(f"d_w0{e}") for e in range(4)]
        for n in small:
            m_rw = sp.dma(ye.dma_start, small[n][:], a[n], st_r)
        m_z = pool.do(ge.memset, zero[:], 0.0)
        sp.wait(m_z)
        m_zx = sp.dma(ye.dma_start, xs.rearrange("(n p) d -> p n d", p=128), zero[:, None, :].broadcast_to([128, NE, 128]), stream("d_zx"))
        for e in range(4):
            sp.dma(ye.dma_start, w1[:, 2048 * e:2048 * e + 2048], a["w1"][:, 2 * e:2 * e + 2, :].rearrange("p e n -> p (e n)"), st_w[e])
            m_w = sp.dma(ye.dma_start, w2[:, 1024 * e:1024 * e + 1024], a["w2"][:, 2 * e:2 * e + 2, :, :].rearrange("p e j n -> p (e j n)"), st_w[e])
            st_w[e].append(m_w)
        exp_steps = exponentials(nc, ph, g)
        one["load"]()
        xn = sb(ph, "xn0", [128, 32, 128])
        xT = [sb(ph, f"xT0{i}", [128, 1024]) for i in range(2)]
        lg = sb(ph, "lg", [128, 8, 8])
        m8 = sb(ph, "m8", [128, 8, 8])
        i8 = sb(ph, "i8", [128, 8, 8], U32)
        fi = sb(ph, "fi", [128, 8])
        nm = sb(ph, "nm", [128, 8])
        ex = sb(ph, "ex", [128, 8, 8])
        sm = sb(ph, "sm", [128, 8])
        share = one["share"]
        oh = sb(ph, "oh", [128, 32, 8])
        f = {"xT": [(), ()], "small": ()}

        def normal(c):
            xc = x[:, 8 * c:8 * c + 8, :]
            xnc = xn[:, 8 * c:8 * c + 8, :]
            m = yield from g["layernorm_steps"](xc, xnc, 8, 1e-5, [x_ready[c]])
            m_t = g["transposed"](xnc, xT[c % 2], 8, m, f["xT"][c % 2])
            placed[c] = m_t
            yield

        def route(c):
            s = take_s()
            pe.wait(placed[c], m_rw)
            for i in range(8):
                m = pe.do(te.matmul, S[s][:, 8 * i:8 * i + 8], xT[c % 2][:, 128 * i:128 * i + 128], rw[:],
                          start=True, stop=True, inc=(i == 7))
            f["xT"][c % 2] = (m,)
            dve.wait(m, *f["small"])
            m = dve.do(ve.tensor_tensor, lg[:], S[s][:, 0:64].rearrange("p (n e) -> p n e", e=8),
                       rb[:, None, :].broadcast_to([128, 8, 8]), ALU.add)
            s_free[s] = (m,)
            dve.wait(m)
            for i in range(8):
                m = dve.do(ve.max, m8[:, i, :], lg[:, i, :])
            dve.wait(m)
            for i in range(8):
                m = dve.do(ve.max_index, i8[:, i, :], m8[:, i, :], lg[:, i, :])
            m_n = dve.do(ve.tensor_scalar, nm[:], m8[:, :, 0], -1.0, None, ALU.mult)
            dve.wait(m)
            m_i = dve.do(ve.tensor_copy, fi[:], i8[:, :, 0])
            act.wait(m_n)
            for i in range(8):
                m = act.do(se.activation, ex[:, i, :], lg[:, i, :], ACT.Exp, bias=nm[:, i:i + 1])
            yield
            dve.wait(m)
            m = dve.do(ve.tensor_reduce, sm[:], ex[:], AX.X, ALU.add)
            dve.wait(m)
            dve.do(ve.reciprocal, share[:, 8 * c:8 * c + 8], sm[:])
            dve.wait(m_i)
            for i in range(8):
                m = dve.do(ve.tensor_scalar, oh[:, 8 * c + i, :], iota[:], fi[:, i:i + 1], None, ALU.is_equal)
            f["small"] = (m,)
            placed["oh"] = m
            yield

        placed = {}
        for _ in normal(0):
            pass
        for c in range(B):
            run_beside(normal(c + 1) if c + 1 < B else (), route(c), 0, 1.0)
        m_oh = placed["oh"]

        def wide(n, w=256, dt=F32):
            return sb(ph, n, [128, w], dt)

        def step(fn, *args):
            m = dve.do(fn, *args)
            dve.wait(m)
            return m

        ohf = oh[:].rearrange("p n e -> p (n e)")
        s = take_s()
        pe.wait(m_oh)
        pe.do(te.matmul, S[s][:, 0:256], small["tri"][:], ohf, start=True, stop=True, inc=False)
        m = pe.do(te.matmul, S[s][:, 512:768], small["one"][:], ohf, start=True, stop=True)
        tot, sc = wide("tot"), [wide("scn0"), wide("scn1")]
        dve.wait(m)
        dve.do(ve.tensor_copy, tot[:], S[s][:, 512:768])
        step(ve.tensor_copy, sc[0][:], S[s][:, 512:768])
        k = 0
        for d in (8, 16, 32, 64, 128):
            dve.do(ve.tensor_copy, sc[1 - k][:, 0:d], sc[k][:, 0:d])
            step(ve.tensor_tensor, sc[1 - k][:, d:256], sc[k][:, d:256], sc[k][:, 0:256 - d], ALU.add)
            k = 1 - k
        count = sc[k][:, 248:256]
        more, nt, upn, cs, st8 = wide("more"), wide("nt", 8), wide("upn", 64), wide("cs", 8), wide("st8", 8)
        step(ve.tensor_tensor, more[:].rearrange("p (e k) -> p e k", e=8), count[:, :, None].broadcast_to([128, 8, 32]),
             small["thr"][:].rearrange("p (e k) -> p e k", e=8), ALU.is_gt)
        step(ve.tensor_reduce, nt[:], more[:].rearrange("p (e k) -> p e k", e=8), AX.X, ALU.add)
        step(ve.tensor_tensor, upn[:].rearrange("p (e k) -> p e k", e=8), nt[:, None, :].broadcast_to([128, 8, 8]),
             small["upto"][:].rearrange("p (e k) -> p e k", e=8), ALU.mult)
        step(ve.tensor_reduce, cs[:], upn[:].rearrange("p (e k) -> p e k", e=8), AX.X, ALU.add)
        step(ve.tensor_tensor, st8[:], cs[:], nt[:], ALU.subtract)
        step(ve.tensor_scalar, st8[:], st8[:], 128.0, None, ALU.mult)
        w = sc[1 - k]
        step(ve.tensor_tensor, w[:], sc[k][:], tot[:], ALU.subtract)
        m = step(ve.tensor_tensor, w[:], w[:], S[s][:, 0:256], ALU.add)
        s_free[s] = (m,)
        w3 = w[:].rearrange("p (n e) -> p n e", e=8)
        step(ve.tensor_tensor, w3, w3, st8[:, None, :].broadcast_to([128, 32, 8]), ALU.add)
        step(ve.tensor_tensor, w[:], w[:], ohf, ALU.mult)
        pos, posi = wide("pos", 32), one["posi"]
        step(ve.tensor_reduce, pos[:], w3, AX.X, ALU.add)
        m_pos = step(ve.tensor_copy, posi[:], pos[:])
        past, et, eti = wide("past", 7 * NE), wide("et", NE), wide("eti", NE, U32)
        p3 = past[:].rearrange("p (t e) -> p t e", e=7)
        step(ve.tensor_tensor, p3, small["tix"][:].rearrange("p (t e) -> p t e", e=7), cs[:, None, 0:7].broadcast_to([128, NE, 7]), ALU.is_ge)
        step(ve.tensor_reduce, et[:], p3, AX.X, ALU.add)
        m_et = step(ve.tensor_copy, eti[:], et[:])

        st_s = stream("d_sc0")
        pool.wait(m_pos, m_zx)
        for n in range(NT):
            m_sc = pool.indirect(ge.indirect_dma_start, xs, bass.IndirectOffsetOnAxis(posi[:, n:n + 1], 0), xn[:, n, :], None, st_s)

        one["prepare"]()
        for _ in range(EXP):
            next(exp_steps)
        NX, NH = 6, 4
        xg = [sb(ph, f"xg{i}", [128, 128]) for i in range(NX)]
        xgT = [sb(ph, f"xgT{i}", [128, 128]) for i in range(NH)]
        th = [sb(ph, f"th{i}", [128, 512]) for i in range(2)]
        uu = [sb(ph, f"uu{i}", [128, 512]) for i in range(2)]
        hh = [sb(ph, f"hh{i}", [128, 512]) for i in range(NH)]
        hT = [sb(ph, f"hT{i}", [128, 512]) for i in range(2)]
        yo = [sb(ph, f"yo{i}", [128, 128]) for i in range(4)]
        st_x = [stream(f"d_xg{i}") for i in range(NX)]
        st_y = [stream(f"d_yo{i}") for i in range(4)]
        xg_free, xgT_free, th_free, hh_free, hT_free, y_free = [()] * NX, [()] * NH, [()] * 2, [()] * NH, [()] * 2, [()] * 4
        loaded, expert = {}, {}

        def load(t):
            sp.wait(m_sc, *xg_free[t % NX])
            loaded[t] = sp.dma(ye.dma_start, xg[t % NX][:], xs[128 * t:128 * t + 128, :], st_x[t % NX])

        def turn(t):
            o = take_a()
            pe.wait(loaded[t])
            m = pe.do(te.transpose, A[o][:, 0:128], xg[t % NX][:], ident[:])
            xg_free[t % NX] = (m,)
            act.wait(m, *xgT_free[t % NH])
            m = act.do(se.activation, xgT[t % NH][:], A[o][:, 0:128], ACT.Copy)
            a_free[o] = (m,)
            return m

        def up(t, m):
            def expert_of():
                expert[t] = te.value_load(eti[0:1, t:t + 1], min_val=0, max_val=7)

            def part(dst, c):
                return te.matmul(dst, xgT[t % NH][:], w1[:, bass.ds(expert[t] * 1024 + c, 512)], start=True, stop=True)

            s = take_s()
            pe.wait(m, m_et)
            pe.do(expert_of, inc=False)
            for c in (0, 512):
                m = pe.do(part, S[s][:, c:c + 512], c, inc=(c == 512))
            xgT_free[t % NH] = (m,)
            q = t % 2
            act.wait(m, *th_free[q])
            m = act.do(se.activation, th[q][:], S[s][:, 0:512], ACT.Tanh, scale=0.5)
            dve.wait(m)
            m = dve.do(ve.scalar_tensor_tensor, uu[q][:], th[q][:], 1.0, S[s][:, 0:512], ALU.add, ALU.mult)
            dve.wait(m, *hh_free[t % NH])
            m = dve.do(ve.tensor_tensor, hh[t % NH][:], uu[q][:], S[s][:, 512:1024], ALU.mult)
            th_free[q] = s_free[s] = (m,)
            return m

        def across(t, m):
            s = take_s()
            pe.wait(m)
            for j in range(4):
                m = pe.do(te.transpose, S[s][:, 128 * j:128 * j + 128], hh[t % NH][:, 128 * j:128 * j + 128], ident[:], inc=(j == 3))
            hh_free[t % NH] = (m,)
            act.wait(m, *hT_free[t % 2])
            m = act.do(se.activation, hT[t % 2][:], S[s][:, 0:512], ACT.Copy)
            s_free[s] = (m,)
            return m

        def down(t, m):
            def part(dst, j):
                return te.matmul(dst, hT[t % 2][:, 128 * j:128 * j + 128], w2[:, bass.ds(expert[t] * 512 + 128 * j, 128)],
                                 start=(j == 0), stop=(j == 3))

            o = take_a()
            pe.wait(m)
            for j in range(4):
                m = pe.do(part, A[o][:, 0:128], j, inc=(j == 3))
            hT_free[t % 2] = (m,)
            dve.wait(m, *y_free[t % 4])
            m = dve.do(ve.tensor_copy, yo[t % 4][:], A[o][:, 0:128])
            a_free[o] = (m,)
            sp.wait(m)
            y_free[t % 4] = (sp.dma(ye.dma_start, ys[128 * t:128 * t + 128, :], yo[t % 4][:], st_y[t % 4]),)

        for e in range(4):
            pe.wait(st_w[e].pop())
        for t in range(NX - 1):
            load(t)
        q1, q2, q3 = [], [], []
        for t in range(NE + DD):
            if t < NE:
                q1.append(turn(t))
            if 0 <= t - 1 < NE:
                q2.append(up(t - 1, q1.pop(0)))
            if 0 <= t - DA < NE:
                q3.append(across(t - DA, q2.pop(0)))
            if t >= DD and t - DD < NE:
                down(t - DD, q3.pop(0))
            if t + NX - 1 < NE:
                load(t + NX - 1)
            if t % 2:
                next(exp_steps, None)
        for _ in exp_steps:
            pass

        m_h = dve.do(ve.tensor_scalar, share[:], share[:], 0.5, None, ALU.mult)
        pool.wait(*[m for y in y_free for m in y])
    g["barrier"]()

    yg, posi = one["yg"], one["posi"]
    st_g = [stream(f"d_yg{i}") for i in range(8)]
    x_done, got = {}, {}

    def gather(n):
        pool.wait(x_done.get(n - 8))
        got[n] = pool.indirect(ge.indirect_dma_start, yg[:, n % 8, :], None, ys, bass.IndirectOffsetOnAxis(posi[:, n:n + 1], 0), st_g[n % 8])

    def add(n):
        dve.wait(got[n], m_h)
        x_done[n] = dve.do(ve.scalar_tensor_tensor, x[:, n, :], yg[:, n % 8, :], share[:, n:n + 1], x[:, n, :], ALU.mult, ALU.add)
        x_ready[n // 8] = x_done[n]

    def batch(b):
        for n in range(8 * b, 8 * b + 12):
            if n < 8 * b + 8:
                gather(n)
            if n >= 8 * b + 4:
                add(n - 4)
            yield

    for n in range(8):
        gather(n)
    for n in range(8):
        add(n)
    return {0: batch(1), 2: batch(2), 3: batch(3)}


def attn1(nc, ctx, g):
    pe, dve, act, pool, sp = (g[k] for k in ("pe", "dve", "act", "pool", "sp"))
    te, ve, se, ge, ye = (g[k] for k in ("te", "ve", "se", "ge", "ye"))
    sb, S, A, take_s, take_a, s_free, a_free = (g[k] for k in ("sb", "S", "A", "take_s", "take_a", "s_free", "a_free"))
    x, x_ready, a, stream, ident = g["x"], g["x_ready"], g["a"], g["stream"], g["ident"]
    one, rest = g["one"], g["rest"]
    with ExitStack() as ph:
        wt, w3, bias, b3, m3, bo, tp = (one[n] for n in ("wt", "w3", "bias", "b3", "m3", "bo", "tp"))
        m_w, m_b, m_tp = one["m_w"], one["m_b"], one["m_tp"]
        xn = sb(ph, "xn1", [128, 8, 128])
        xT = sb(ph, "xT1", [128, T])
        gT = [sb(ph, f"gT{i}", [128, T]) for i in range(2)]
        V = [sb(ph, f"Va{i}", [128, 8, 16, 9]) for i in range(2)]
        X3 = sb(ph, "X3", [96, T])
        H3, F3 = sb(ph, "H3", [96, T], F32R), sb(ph, "F3", [96, T], F32R)
        K3 = [sb(ph, f"K3{i}", [96, T], F32R) for i in range(3)]
        Q3 = sb(ph, "Q3", [96, 12, T], F32R)
        sc = [sb(ph, f"sc{i}", [128, 2, 320]) for i in range(NS)]
        pr = [sb(ph, f"pr{i}", [128, 2, 384]) for i in range(NP)]
        pt = [sb(ph, f"pt{i}", [128, 2, 384]) for i in range(NT3)]
        mn = [sb(ph, f"mn{i}", [128, 2]) for i in range(NS)]
        rec = sb(ph, "rec1", [128, 4, 4])
        ao = sb(ph, "ao", [128, 512])
        at = sb(ph, "at1", [128, 8, 128])
        ga = sb(ph, "ga", [128, 512])
        for v in V:
            m_one = pool.do(ge.memset, v[:, :, :, 8:9], 1.0)
        for t in pr:
            m_zero = pool.do(ge.memset, t[:], 0.0)
        for h in range(0, 12, 4):
            m_z3 = pool.do(ge.memset, Q3[:, h:h + 4, :].bitcast(F32), 0.0)
        for o in A:
            m_a = dve.do(ve.memset, o[:], 0.0)
        pe.wait(m_a)
        st_q = [stream(f"d_q3{i}") for i in range(3)]
        f = {"xn": (), "xT": (), "X3": (), "F3": (), "at": [(), ()], "ao": (), "ga": (), "g": [(), ()], "v": [(), ()], "kq": [()] * 3}
        ready = {}

        def prep(b):
            p = b % 2
            xb = x[:, 8 * b:8 * b + 8, :]
            m_n = yield from g["layernorm_steps"](xb, xn, 8, 1e-5, [x_ready[b]], f["xn"])
            yield
            pool.wait(m_n)
            ready["x", b] = pool.do(ge.tensor_tensor, xb, xb, bo[:, None, :].broadcast_to([128, 8, 128]), ALU.add)
            m_t = ready["xT", b] = g["transposed"](xn, xT, 8, m_n, f["xT"])
            f["xn"] = (m_t,)
            yield
            s = take_s()
            pe.wait(m_t, m_w)
            for i in range(2):
                m = pe.do(te.matmul, S[s][:, 512 * i:512 * i + 512], wt["ug"][:], xT[:, 512 * i:512 * i + 512], start=True, stop=True, inc=(i == 1))
            act.wait(m, m_b, *f["g"][p])
            ready["g", b] = act.do(se.activation, gT[p][:], S[s][:], ACT.Tanh, bias=bias[:, 0:1], scale=0.5)
            s_free[s] = (ready["g", b],)
            yield
            dve.wait(ready["g", b])
            ready["g", b] = dve.do(ve.tensor_scalar, gT[p][:], gT[p][:], 1.0, 0.5, ALU.add, ALU.mult)
            yield
            s = take_s()
            for i in range(8):
                m = pe.do(te.matmul, S[s][:, 128 * i:128 * i + 128], xT[:, 128 * i:128 * i + 128], wt["uv"][:],
                          start=True, stop=True, inc=(i == 7))
            dve.wait(m, m_one, *f["v"][p])
            ready["v", b] = dve.do(ve.tensor_copy, V[p][:, :, :, 0:8], S[s][:].rearrange("p (n h d) -> p n h d", n=8, h=16))
            s_free[s] = (ready["v", b],)
            yield

        def prep_group(w):
            b, r, z = w // 4, w % 4, w % 3
            for n in ("k", "q"):
                s = take_s()
                pe.wait(ready["xT", b])
                for i in range(2):
                    m = pe.do(te.matmul, S[s][0:96, 512 * i:512 * i + 512], w3["u" + n + "3"][:, r, :], xT[:, 512 * i:512 * i + 512],
                              start=True, stop=True, inc=(i == 1))
                act.wait(m, m_b, *f["X3"])
                for t in (X3, H3):
                    m = act.do(se.activation, t[:], S[s][0:96, :], ACT.Identity, bias=b3["b" + n + "3"][:, r:r + 1],
                               scale=SCALE1 if n == "q" else 1.0)
                s_free[s] = (m,)
                yield
                dve.wait(m, *(f["kq"][z] if n == "k" else f["F3"]))
                m = dve.do(ve.scalar_tensor_tensor, K3[z][:] if n == "k" else F3[:], H3[:].bitcast(F32),
                           m3["m" + n + "3"][:, 0:1], X3[:], ALU.mult, ALU.add)
                f["X3"] = (m,)
                if n == "k":
                    ready["k", w] = m
                else:
                    sp.wait(m, m_z3, *f["kq"][z])
                    for h in range(4):
                        m = sp.dma(ye.dma_start, Q3[24 * h:24 * h + 24, 4 * z + h, :].bitcast(F32),
                                   F3[24 * h:24 * h + 24, :].bitcast(F32), st_q[z])
                    f["F3"] = (m,)
                    ready["q", w] = m
                yield
            if r == 3:
                f["xT"] = ((pe.sem, pe.n),)

        k = [0, 0, 0]
        tails = []

        def scores(w, qt, hp, oa):
            r, z = w % 4, w % 3
            j0 = max(0, 192 - 128 * qt)
            n = 320 - j0
            s = take_s()
            c = k[0]
            k[0] += 1
            kk = 128 * qt - 192 + j0
            for i in range(2):
                h = 4 * r + 2 * hp + i
                m = pe.do(te.matmul, S[s][:, 512 * i:512 * i + n], Q3[:, 4 * z + 2 * hp + i, 128 * qt:128 * qt + 128], K3[z][:, kk:kk + n], start=True, stop=True)
                dve.wait(m, m_tp, *sc_free[c % NS][i])
                m = dve.do(ve.tensor_tensor_reduce, out=sc[c % NS][:, i, 0:n], in0=S[s][:, 512 * i:512 * i + n], in1=tp[:, h, j0:320],
                           scale=1.0, scalar=3e38, op0=ALU.add, op1=ALU.min, accum_out=mn[c % NS][:, i:i + 1])
                act.wait(m, m_zero, *pr_free[c % NP])
                m_e = act.do(se.activation, pr[c % NP][:, i, 384 - n:384], sc[c % NS][:, i, 0:n], ACT.Exp, bias=mn[c % NS][:, i:i + 1], scale=-1.0)
                sc_free[c % NS][i] = (m_e,)
            s_free[s] = (m,)
            return (w, qt, hp, oa, c % NP, m_e)

        def turn(w, qt, hp, oa, c, m):
            lo = max(0, 2 - qt)
            s = take_s()
            pe.wait(m)
            for i in range(2):
                for j in range(lo, 3):
                    o = 384 * i + 128 * j
                    m = pe.do(te.transpose, S[s][:, o:o + 128], pr[c][:, i, 128 * j:128 * j + 128], ident[:], inc=(i == 1 and j == 2))
            pr_free[c] = (m,)
            t = k[1] % NT3
            k[1] += 1
            q, fn = (act, se.copy) if k[1] % EVAC == 0 else (dve, ve.tensor_copy)
            q.wait(m, *pt_free[t])
            src = S[s][:, 0:768].rearrange("p (i n) -> p i n", i=2)
            if q is act:
                m = act.do(se.activation, pt[t][:, :, 128 * lo:384], src[:, :, 128 * lo:384], ACT.Copy)
            else:
                m = dve.do(ve.tensor_copy, pt[t][:, :, 128 * lo:384], src[:, :, 128 * lo:384])
            s_free[s] = (m,)
            return (w, qt, oa, t, lo, m)

        def values(one_pair, other):
            w, qt, oa, _, lo, _ = one_pair
            b, r = w // 4, w % 4
            pe.wait(one_pair[5], other[5])
            for j in range(lo, 3):
                for h in range(4):
                    m = pe.do(te.matmul, A[oa][32 * h:32 * h + 9, 128 * (qt % 4):128 * (qt % 4) + 128], V[b % 2][:, qt - 2 + j, 4 * r + h, :],
                              pt[(one_pair, other)[h // 2][3]][:, h % 2, 128 * j:128 * j + 128],
                              start=(j == lo), stop=(j == 2), tile_position=(0, 32 * h), inc=(j == 2))
            pt_free[one_pair[3]] = pt_free[other[3]] = (m,)
            if qt % 4 == 3:
                tails.append(tail(w, qt // 4, oa, m))

        def tail(w, i, oa, m):
            b, r = w // 4, w % 4
            act.wait(m, *f["ao"])
            m = act.do(se.activation, ao[:], A[oa][:], ACT.Copy)
            a_free[oa] = (m,)
            if (r, i) == (3, 1):
                f["v"][b % 2] = (m,)
            yield
            s = take_s()
            pe.wait(m)
            for j in range(4):
                m = pe.do(te.transpose, S[s][:, 128 * j:128 * j + 128], ao[:, 128 * j:128 * j + 128], ident[:], inc=(j == 3))
            f["ao"] = (m,)
            o = S[s][:, 0:512].rearrange("p (n h d) -> p n h d", n=4, h=4)
            dve.wait(m)
            m = dve.do(ve.reciprocal, rec[:, :, :, None], o[:, :, :, 8:9])
            dve.wait(m, *f["at"][i])
            m = dve.do(ve.tensor_tensor, at[:, 4 * i:4 * i + 4, 32 * r:32 * r + 32].rearrange("p n (h d) -> p n h d", d=8),
                       o[:, :, :, 0:8], rec[:, :, :, None].broadcast_to([128, 4, 4, 8]), ALU.mult)
            s_free[s] = (m,)
            if r < 3:
                return
            yield
            s = take_s()
            pe.wait(m)
            for j in range(4):
                m = pe.do(te.transpose, S[s][:, 128 * j:128 * j + 128], at[:, 4 * i + j, :], ident[:], inc=(j == 3))
            f["at"][i] = (m,)
            dve.wait(m, ready["g", b], *f["ga"])
            m_ga = dve.do(ve.scalar_tensor_tensor, ga[:], S[s][:, 0:512], bias[:, 1:2], gT[b % 2][:, 512 * i:512 * i + 512], ALU.add, ALU.mult)
            s_free[s] = (m_ga,)
            yield
            s = take_s()
            pe.wait(m_ga)
            for j in range(4):
                m = pe.do(te.matmul, S[s][:, 128 * j:128 * j + 128], ga[:, 128 * j:128 * j + 128], wt["uo"][:], start=True, stop=True, inc=(j == 3))
            f["ga"] = (m,)
            dve.wait(m, ready["x", b])
            xb = x[:, 8 * b + 4 * i:8 * b + 4 * i + 4, :].rearrange("p n d -> p (n d)")
            m = dve.do(ve.tensor_tensor, xb, xb, S[s][:, 0:512], ALU.add)
            s_free[s] = (m,)
            if i:
                f["g"][b % 2] = (m_ga,)
                x_ready[b] = m

        pr_free, pt_free, sc_free = [()] * NP, [()] * NT3, [[(), ()] for _ in range(NS)]
        first, two = [], []

        def advance(last=False):
            if tails:
                try:
                    next(tails[0])
                except StopIteration:
                    tails.pop(0)
            if first and (last or len(first) > LAG1):
                two.append(turn(*first.pop(0)))
            if len(two) >= (2 if last else LAG2):
                values(two.pop(0), two.pop(0))

        def attend(w):
            for qt in range(8):
                if qt % 4 == 0:
                    oa = take_a()
                if qt == 0:
                    pe.wait(ready["k", w], ready["q", w], ready["v", w // 4])
                for hp in range(2):
                    first.append(scores(w, qt, hp, oa))
                    advance()
                    yield
            f["kq"][w % 3] = ((pe.sem, pe.n),)

        def ahead(w):
            if w in rest:
                yield from rest[w]
            if w + 2 < 4 * B:
                yield from prep_group(w + 2)
            if w % 4 == 1 and w // 4 + 1 < B:
                yield from prep(w // 4 + 1)

        for part in (prep(0), prep_group(0), prep_group(1)):
            for _ in part:
                pass
        for w in range(4 * B):
            run_beside(attend(w), ahead(w), *(PACE1[w % 4 == 1]))
        while first or two or tails:
            advance(True)
    g["barrier"]()


def ffn1(nc, ctx, g):
    pe, dve, act, pool, sp = (g[k] for k in ("pe", "dve", "act", "pool", "sp"))
    te, ve, se, ge, ye = (g[k] for k in ("te", "ve", "se", "ge", "ye"))
    sb, S, A, take_s, take_a, s_free, a_free = (g[k] for k in ("sb", "S", "A", "take_s", "take_a", "s_free", "a_free"))
    x, x_ready, a, stream, ident, R = (g[k] for k in ("x", "x_ready", "a", "stream", "ident", "R"))
    with ExitStack() as ph:
        st = stream("d_f1")
        aw = sb(ph, "aw", [128, 128])
        cols = sb(ph, "cols", [128, 3])
        gam, bet = sb(ph, "gam", [128, 128]), sb(ph, "bet", [128, 128])
        mw, mb = sb(ph, "mw", [128, 8]), sb(ph, "mb", [128, 8])
        e1 = sb(ph, "e1", [128, 8, 256])
        e2 = sb(ph, "e2", [128, 8, 2, 128])
        b1 = sb(ph, "b1", [128, 8, 2])
        b2 = sb(ph, "b2", [8, 128])
        gca, gcb = sb(ph, "gca", [128, 128]), sb(ph, "gcb", [128, 128])
        iota = sb(ph, "iota1", [128, 8])
        for n, t in (("aw", aw), ("cols", cols), ("gam", gam), ("bet", bet), ("mw", mw), ("mb", mb), ("iota", iota), ("b1", b1),
                     ("b2", b2), ("gca", gca), ("gcb", gcb)):
            m_w = sp.dma(ye.dma_start, t[:], a[n], st)
        st_e = stream("d_f1e")
        sp.dma(ye.dma_start, e1[:], a["e1"], st_e)
        m_e = sp.dma(ye.dma_start, e2[:], a["e2"], st_e)

        flat = lambda t: t[:].rearrange("p n d -> p (n d)")
        ready = {}

        n1 = [sb(ph, f"n1{i}", [128, 4, 128]) for i in range(2)]
        n2 = sb(ph, "n2", [128, 4, 128])
        nT = [sb(ph, f"nT{i}", [128, 512]) for i in range(2)]
        lg = sb(ph, "lg1", [128, 4, 8])
        m8 = sb(ph, "m81", [128, 4, 8])
        i8 = sb(ph, "i81", [128, 4, 8], U32)
        fi = sb(ph, "fi1", [128, 4, 2])
        dd = sb(ph, "dd", [128, 4])
        w01 = sb(ph, "w01", [128, 4, 2])
        wt2 = sb(ph, "wt2", [128, 8])
        wd = [sb(ph, f"wd{i}", [128, 4, 8]) for i in range(2)]
        wdT = sb(ph, "wdT", [8, 512])
        h = [sb(ph, f"h1{i}", [128, 2, 512]) for i in range(2)]
        acc = [sb(ph, f"acc{i}", [128, 4, 128]) for i in range(2)]
        ab = [sb(ph, f"ab{i}", [128, 512]) for i in range(2)]
        mo, mr, gt, df = (sb(ph, n, [128, 512]) for n in ("mo", "mr", "gt", "df"))
        h_free = [(), ()]
        pend = []

        def start_(c):
            p = c % 2
            xc = x[:, 4 * c:4 * c + 4, :]
            was = ((pe.sem, pe.n), (dve.sem, dve.n))
            m_n1 = yield from g["layernorm_steps"](xc, n1[p], 4, 1e-5, [x_ready[c // 2]], was)
            dve.wait(m_n1)
            m = yield from g["layernorm_steps"](n1[p], n2, 4, 1e-5, [m_n1], ())
            if c == 0:
                dve.wait(m_w)
                dve.do(ve.tensor_scalar, cols[:, 1:2], cols[:, 1:2], 0.5, None, ALU.mult)
            dve.wait(m)
            m = dve.do(ve.tensor_tensor, n2[:], n2[:], gam[:, None, :].broadcast_to([128, 4, 128]), ALU.mult)
            dve.wait(m)
            m = dve.do(ve.tensor_tensor, n2[:], n2[:], bet[:, None, :].broadcast_to([128, 4, 128]), ALU.add)
            yield
            m_t = g["transposed"](n2, nT[p], 4, m, was[:1])
            yield
            s = take_s()
            pe.wait(m_t)
            for i in range(4):
                m = pe.do(te.matmul, S[s][:, 8 * i:8 * i + 8], nT[p][:, 128 * i:128 * i + 128], mw[:],
                          start=True, stop=True, inc=False)
            m = pe.do(te.matmul, S[s][:, 512:1024], aw[:], nT[p][:], start=True, stop=True)
            act.wait(m, *was)
            m_ab = act.do(se.activation, ab[p][:], S[s][:, 512:1024], ACT.Gelu, bias=cols[:, 0:1])
            dve.wait(m)
            m = dve.do(ve.tensor_tensor, lg[:], S[s][:, 0:32].rearrange("p (n e) -> p n e", e=8),
                       mb[:, None, :].broadcast_to([128, 4, 8]), ALU.add)
            s_free[s] = (m, m_ab)
            yield
            dve.wait(m)
            for i in range(4):
                m = dve.do(ve.max, m8[:, i, :], lg[:, i, :])
            dve.wait(m)
            for i in range(4):
                m_i = dve.do(ve.max_index, i8[:, i, :], m8[:, i, :], lg[:, i, :])
            m = dve.do(ve.tensor_tensor, dd[:], m8[:, :, 0], m8[:, :, 1], ALU.subtract)
            dve.wait(m_i)
            m_i = dve.do(ve.tensor_copy, fi[:], i8[:, :, 0:2])
            act.wait(m)
            m = act.do(se.activation, dd[:], dd[:], ACT.Tanh, scale=0.5)
            yield
            dve.wait(m)
            m = dve.do(ve.tensor_scalar, w01[:, :, 0], dd[:], 0.5, 0.5, ALU.mult, ALU.add)
            m = dve.do(ve.tensor_scalar, w01[:, :, 1], dd[:], -0.5, 0.5, ALU.mult, ALU.add)
            dve.wait(m, m_i)
            for i in range(4):
                m = dve.do(ve.tensor_scalar, wt2[:], iota[:], fi[:, i, 0:1], w01[:, i, 0:1], ALU.is_equal, ALU.mult)
                m_2 = dve.do(ve.tensor_scalar, wd[p][:, i, :], iota[:], fi[:, i, 1:2], w01[:, i, 1:2], ALU.is_equal, ALU.mult)
                dve.wait(m_2)
                m = dve.do(ve.tensor_tensor, wd[p][:, i, :], wd[p][:, i, :], wt2[:], ALU.add)
                dve.wait(m)
            yield
            s = take_s()
            pe.wait(m)
            for i in range(4):
                m = pe.do(te.transpose, S[s][0:8, 128 * i:128 * i + 128], wd[p][:, i, :], ident[:], inc=(i == 3))
            dve.wait(m)
            m = dve.do(ve.tensor_copy, wdT[:], S[s][0:8, 0:512])
            s_free[s] = (m,)
            yield
            s = take_s()
            pe.wait(m)
            for i in range(4):
                m = pe.do(te.matmul, S[s][:, 512 + 128 * i:640 + 128 * i], wdT[:, 128 * i:128 * i + 128], b2[:], start=True, stop=True, inc=(i == 3))
            dve.wait(m)
            m = dve.do(ve.tensor_copy, flat(acc[p]), S[s][:, 512:1024])
            s_free[s] = (m,)
            ready[c] = m_t, m_ab, m

        def down():
            c, e, hb, m_h = pend.pop(0)
            p = c % 2
            o = take_a()
            pe.wait(m_h)
            for i in range(4):
                for j in range(2):
                    m = pe.do(te.matmul, A[o][:, 128 * i:128 * i + 128], h[hb][:, j, 128 * i:128 * i + 128], e2[:, e, j, :],
                              start=(j == 0), stop=(j == 1), inc=(i == 3 and j == 1))
            h_free[hb] = (m,)
            dve.wait(m, (dve.sem, dve.n))
            for i in range(4):
                ai = acc[p][:, i, :]
                m = dve.do(ve.scalar_tensor_tensor, ai, A[o][:, 128 * i:128 * i + 128], wd[p][:, i, e:e + 1], ai, ALU.mult, ALU.add)
            a_free[o] = (m,)
            summed[c] = m

        def finish(c):
            p = c % 2
            m_acc, m_ab = summed[c], ready[c][1]
            s = take_s()
            pe.wait(m_acc)
            for i in range(4):
                m = pe.do(te.transpose, S[s][:, 128 * i:128 * i + 128], acc[p][:, i, :], ident[:], inc=(i == 3))
            dve.wait(m)
            m = dve.do(ve.tensor_copy, mo[:], S[s][:, 0:512])
            s_free[s] = (m,)
            yield
            s = take_s()
            pe.wait(m)
            m = pe.do(te.matmul, S[s][:, 512:1024], R[:], mo[:], start=True, stop=True)
            dve.wait(m)
            m = dve.do(ve.tensor_copy, mr[:], S[s][:, 512:1024])
            s_free[s] = (m,)
            yield
            s = take_s()
            pe.wait(m, m_ab)
            pe.do(te.matmul, S[s][:, 0:512], gca[:], ab[p][:], start=True, stop=False, inc=False)
            m_g = pe.do(te.matmul, S[s][:, 0:512], gcb[:], mr[:], start=False, stop=True)
            dve.wait(m)
            m_d = dve.do(ve.tensor_tensor, df[:], mr[:], ab[p][:], ALU.subtract)
            act.wait(m_g)
            m = act.do(se.activation, gt[:], S[s][:, 0:512], ACT.Tanh, bias=cols[:, 1:2], scale=0.5)
            s_free[s] = (m,)
            yield
            dve.wait(m, m_d)
            m = dve.do(ve.scalar_tensor_tensor, df[:], gt[:], 1.0, df[:], ALU.add, ALU.mult)
            dve.wait(m)
            m = dve.do(ve.scalar_tensor_tensor, df[:], df[:], 0.5, ab[p][:], ALU.mult, ALU.add)
            yield
            s = take_s()
            pe.wait(m)
            for i in range(4):
                m = pe.do(te.transpose, S[s][:, 512 + 128 * i:640 + 128 * i], df[:, 128 * i:128 * i + 128], ident[:], inc=(i == 3))
            xc = x[:, 4 * c:4 * c + 4, :].rearrange("p n d -> p (n d)")
            m_1 = dve.do(ve.tensor_tensor, xc, xc, flat(n1[p]), ALU.add)
            dve.wait(m, m_1)
            m = dve.do(ve.tensor_tensor, xc, xc, S[s][:, 512:1024], ALU.add)
            s_free[s] = (m,)
            x_out[c] = m
            yield

        x_out, summed = {}, {}

        def experts(c):
            m_t = ready[c][0]
            for e in range(8):
                hb = e % 2
                s = take_s()
                pe.wait(m_t, m_e)
                for j in range(2):
                    m = pe.do(te.matmul, S[s][:, 512 * j:512 * j + 512], e1[:, e, 128 * j:128 * j + 128], nT[c % 2][:],
                              start=True, stop=True, inc=(j == 1))
                act.wait(m, *h_free[hb])
                for j in range(2):
                    m = act.do(se.activation, h[hb][:, j, :], S[s][:, 512 * j:512 * j + 512], ACT.Gelu, bias=b1[:, e, j:j + 1])
                s_free[s] = (m,)
                if pend:
                    down()
                pend.append((c, e, hb, m))
                yield

        def beside(c):
            if c:
                yield from finish(c - 1)
            if c < 7:
                yield from start_(c + 1)

        for _ in start_(0):
            pass
        for c in range(8):
            run_beside(experts(c), beside(c), *(PACEF[0] if c < 2 else PACEF[1]))
        down()
        for _ in finish(7):
            pass
        for b in range(B):
            x_ready[b] = x_out[2 * b + 1]


def constants():
    inv = 1.0 / 10000.0 ** (np.arange(0, 32, 2, dtype=np.float32) / 32)
    f = np.outer(np.arange(T, dtype=np.float32), inv)
    emb = np.concatenate([f, f], -1)
    c, s = np.cos(emb).T.astype(np.float32), np.sin(emb).T.astype(np.float32)
    s = np.concatenate([-s[:16], s[16:]], 0)
    k = np.arange(128)
    return {
        "ident": np.eye(128, dtype=np.float32),
        "cos": np.ascontiguousarray(np.tile(c, (4, 1))),
        "sin": np.ascontiguousarray(np.tile(s, (4, 1))),
        "tri": (k[:, None] < k[None, :]).astype(np.float32),
        "one": np.ones((128, 128), np.float32),
        "thr": spread(np.tile(128.0 * np.arange(32, dtype=np.float32), 8)),
        "upto": spread((np.arange(8)[None, :] <= np.arange(8)[:, None]).astype(np.float32).reshape(64)),
        "tix": spread(np.repeat(np.arange(NE, dtype=np.float32), 7)),
        "iota": np.tile(np.arange(8, dtype=np.float32), (128, 1)),
        "mkq": np.where(k[:, None] > k[None, :], NEG, 0.0).astype(np.float32),
        "mqk": np.where(k[None, :] > k[:, None], NEG, 0.0).astype(np.float32),
    }


def rows(w, n=128):
    out = np.zeros((n,) + w.shape[1:], w.dtype)
    out[:w.shape[0]] = w
    return out


def thrice(w):
    w = w.reshape(w.shape[0], 4, 4, 1, 8)
    return np.broadcast_to(w, w.shape[:3] + (3, 8)).reshape(w.shape[0], 4, 96)


def spread(v):
    return np.broadcast_to(v[None, :], (128, v.shape[0]))


def rotated(w):
    r = w.reshape(w.shape[0], 16, 2, 16)
    return np.ascontiguousarray(r[:, :, ::-1, :]).reshape(w.shape)


def layout(i):
    wq = np.zeros((128, 128), np.float32)
    wq[:, :64] = i["L0_attn_W_q"]
    d = dict(constants())
    d.update({
        "x": i["L0_attn_x"].reshape(B * T, D),
        "wq": wq,
        "wqd": rows(i["L0_attn_W_qdec"]),
        "wkd": rows(i["L0_attn_W_kdec"]),
        "wvd": rows(i["L0_attn_W_vdec"]),
        "wo0": i["L0_attn_W_o"],
        "wkv": i["L0_attn_W_kv"],
        "gkv": rows(i["L0_attn_g_kv"].reshape(32, 1)),
        "wqA": rows(i["L0_attn_W_qrope"]),
        "wqB": rows(rotated(i["L0_attn_W_qrope"])),
        "wkA": i["L0_attn_W_krope"],
        "wkB": rotated(i["L0_attn_W_krope"]),
    })
    w = i["L1_attn_Wqkv"]
    bq = i["L1_attn_bqkv"].reshape(3, 128)
    bg = i["L1_attn_bgate"]
    ext = np.full((16, 640), NEG, np.float32)
    ext[:, [o + 127 for o in OFFS]] = i["L1_attn_pos_bias"].T
    p = np.arange(128)[:, None]
    j = np.arange(320)[None, :]
    d.update({
        "rw": i["L0_ffn_router_w"],
        "rb": spread(i["L0_ffn_router_b"]),
        "w1": i["L0_ffn_w1"].transpose(1, 0, 2),
        "w2": i["L0_ffn_w2"].reshape(8, 4, 128, 128).transpose(2, 0, 1, 3),
        "uq3": thrice(w[0:128].T), "uk3": thrice(w[128:256].T), "uv": w[256:384].T,
        "bq3": thrice(bq[0:1])[0].T, "bk3": thrice(bq[1:2])[0].T,
        "mq3": np.tile(np.repeat(np.float32([0, 0, -1]), 8), 4)[:, None],
        "mk3": np.tile(np.repeat(np.float32([0, -1, 0]), 8), 4)[:, None],
        "ug": i["L1_attn_Wgate"].T, "uo": i["L1_attn_Wout"].T,
        "bias1": np.stack([bg, bq[2]], 1),
        "bo": spread(i["L1_attn_bout"]),
        "tp": ext[:, p - j + 192 + 127].transpose(1, 0, 2),
        "aw": i["L1_ffn_abel_w"],
        "cols": np.stack([i["L1_ffn_abel_b"], np.broadcast_to(i["L1_ffn_gc_b"], (128,)), i["L1_ffn_abel_b"]], 1),
        "gam": spread(i["L1_ffn_ln_gamma"]), "bet": spread(i["L1_ffn_ln_beta"]),
        "mw": i["L1_ffn_moe_gate_w"], "mb": spread(i["L1_ffn_moe_gate_b"]),
        "e1": i["L1_ffn_ew1"].transpose(1, 0, 2),
        "e2": i["L1_ffn_ew2"].reshape(8, 2, 128, 128).transpose(2, 0, 1, 3),
        "b1": i["L1_ffn_eb1"].reshape(8, 2, 128).transpose(2, 0, 1),
        "b2": i["L1_ffn_eb2"],
        "gm": i["L1_ffn_gens"].transpose(1, 0, 2),
        "gca": np.broadcast_to(i["L1_ffn_gc_w"][0:128], (128, 128)),
        "gcb": np.broadcast_to(i["L1_ffn_gc_w"][128:256], (128, 128)),
    })
    return d


def kernel(**inputs):
    import concourse.bacc as bacc
    from concourse.bass_utils import run_bass_kernel_spmd as run

    i = {k: np.asarray(v) for k, v in inputs.items()}
    nc = bacc.Bacc("TRN2", target_bir_lowering=False, num_devices=1)
    arrays = {"in_" + k: np.ascontiguousarray(v) for k, v in layout(i).items()}
    aps = {k[3:]: nc.dram_tensor(k, v.shape, mybir.dt.from_np(v.dtype), kind="ExternalInput").ap() for k, v in arrays.items()}
    out = nc.dram_tensor("out", (B * T, D), F32, kind="ExternalOutput").ap()
    program(nc, aps, out)
    r = run(nc, [arrays], core_ids=[0])
    return r.results[0]["out"].reshape(B, T, D)
```
